# Optimizing a Trainium2 kernel written in Bass

```python
import numpy as np
import jax
import jax.numpy as jnp

def _softmax(x, axis=-1):
    return jax.nn.softmax(x, axis=axis)
def _gelu(x):
    return jax.nn.gelu(x, approximate=True)
def _silu(x):
    return jax.nn.silu(x)
def _sigmoid(x):
    return jax.nn.sigmoid(x)
def _layernorm(x, axis=-1, eps=1e-5):
    m = jnp.mean(x, axis=axis, keepdims=True)
    v = jnp.var(x, axis=axis, keepdims=True)
    return (x - m) / jnp.sqrt(v + eps)
def _scatter_add(tgt, idx, src, axis=0):
    return tgt.at[idx].add(src)
def _segment_sum(src, seg, n):
    return jax.ops.segment_sum(src, seg, n)

kernel_name = 'mk_conv_seq_d1_conv_nchw1024_735131'

def setup_inputs(seed: int = 0):
    np.random.seed(seed)
    _w = jnp.asarray
    def _rec_inputs():
        import jax
        import jax.numpy as jnp
        _gk = jax.random.key(seed)
        x = -0.0003929 + 0.9999 * jax.random.normal(jax.random.fold_in(_gk, 1), (16, 1024, 32, 32), jnp.float32)
        return x
    x = _rec_inputs()
    def _L0_conv_setup():
        import jax, jax.numpy as jnp
        import numpy as np
        import math
        B, CIN, CP, H, W = (16, 1024, 512, 32, 32)
        ORDER = 2
        GAMMA = 0.0001
        EPS = 1e-05

        def _rbf_kernel(t, p, g):
            b, c, h, w = t.shape
            n = c * h * w
            tf = t.reshape(b, n)
            pf = p.reshape(b, n)
            gf = g.reshape(b, n)
            beta = math.exp(-2.0 * GAMMA)
            alphas = [math.sqrt((2.0 * GAMMA) ** o / math.factorial(o) * beta) for o in range(ORDER + 1)]
            t_taylor = jnp.stack([jnp.float32(a) * tf ** o for o, a in enumerate(alphas)], axis=1)
            p_taylor = jnp.stack([jnp.float32(a) * pf ** o for o, a in enumerate(alphas)], axis=1)
            att = jnp.einsum('bkn,bn->bk', p_taylor, gf)
            out = jnp.einsum('bk,bkn->bn', att, t_taylor)
            return out.reshape(b, c, h, w)
        key = jax.random.key(seed)
        k = jax.random.split(key, 5)
        x = jax.random.normal(k[0], (B, CIN, H, W), dtype=jnp.float32)
        s_in = 1.0 / math.sqrt(CIN)
        s_p = 1.0 / math.sqrt(CP)
        Wt = jax.random.normal(k[1], (CP, CIN), dtype=jnp.float32) * s_in
        Wp = jax.random.normal(k[2], (CP, CIN), dtype=jnp.float32) * s_in
        Wg = jax.random.normal(k[3], (CP, CIN), dtype=jnp.float32) * s_in
        Wz = jax.random.normal(k[4], (CIN, CP), dtype=jnp.float32) * s_p
        gn_w = jnp.ones((CIN,), dtype=jnp.float32)
        gn_b = jnp.zeros((CIN,), dtype=jnp.float32)
        return {'x': x, 'Wt': Wt, 'Wp': Wp, 'Wg': Wg, 'Wz': Wz, 'gn_w': gn_w, 'gn_b': gn_b}
    _L0_conv_all = _L0_conv_setup()
    _L0_conv_in = {k: v for k, v in _L0_conv_all.items() if k in ('Wt', 'Wp', 'Wg', 'Wz', 'gn_w', 'gn_b', )}
    del _L0_conv_all

    return {
        "x": x,
        "L0_conv_Wt": _L0_conv_in["Wt"],
        "L0_conv_Wp": _L0_conv_in["Wp"],
        "L0_conv_Wg": _L0_conv_in["Wg"],
        "L0_conv_Wz": _L0_conv_in["Wz"],
        "L0_conv_gn_w": _L0_conv_in["gn_w"],
        "L0_conv_gn_b": _L0_conv_in["gn_b"],
    }

def reference(x, L0_conv_Wt, L0_conv_Wp, L0_conv_Wg, L0_conv_Wz, L0_conv_gn_w, L0_conv_gn_b):
    import jax
    import jax.numpy as jnp
    def _L0_conv_ref(x, Wt, Wp, Wg, Wz, gn_w, gn_b):
        import jax, jax.numpy as jnp
        import numpy as np
        import math
        B, CIN, CP, H, W = (16, 1024, 512, 32, 32)
        ORDER = 2
        GAMMA = 0.0001
        EPS = 1e-05

        def _rbf_kernel(t, p, g):
            b, c, h, w = t.shape
            n = c * h * w
            tf = t.reshape(b, n)
            pf = p.reshape(b, n)
            gf = g.reshape(b, n)
            beta = math.exp(-2.0 * GAMMA)
            alphas = [math.sqrt((2.0 * GAMMA) ** o / math.factorial(o) * beta) for o in range(ORDER + 1)]
            t_taylor = jnp.stack([jnp.float32(a) * tf ** o for o, a in enumerate(alphas)], axis=1)
            p_taylor = jnp.stack([jnp.float32(a) * pf ** o for o, a in enumerate(alphas)], axis=1)
            att = jnp.einsum('bkn,bn->bk', p_taylor, gf)
            out = jnp.einsum('bk,bkn->bn', att, t_taylor)
            return out.reshape(b, c, h, w)
        t = jnp.einsum('oc,bchw->bohw', Wt, x)
        p = jnp.einsum('oc,bchw->bohw', Wp, x)
        g = jnp.einsum('oc,bchw->bohw', Wg, x)
        y = _rbf_kernel(t, p, g)
        z = jnp.einsum('oc,bchw->bohw', Wz, y)
        mu = jnp.mean(z, axis=(1, 2, 3), keepdims=True)
        var = jnp.mean((z - mu) ** 2, axis=(1, 2, 3), keepdims=True)
        zn = (z - mu) * jax.lax.rsqrt(var + EPS)
        zn = zn * gn_w[None, :, None, None] + gn_b[None, :, None, None]
        return zn + x

    def _gn(v, G=32, eps=1e-5):
        B_, C_, H_, W_ = v.shape
        g = v.reshape(B_, G, C_ // G, H_, W_)
        m = jnp.mean(g, axis=(2, 3, 4), keepdims=True)
        s = jnp.var(g, axis=(2, 3, 4), keepdims=True)
        return ((g - m) / jnp.sqrt(s + eps)).reshape(v.shape)

    def _ln_c(v, eps=1e-6):
        m = jnp.mean(v, axis=1, keepdims=True)
        s = jnp.var(v, axis=1, keepdims=True)
        return (v - m) / jnp.sqrt(s + eps)

    def _ln_t(v, eps=1e-5):
        m = jnp.mean(v, axis=-1, keepdims=True)
        s = jnp.var(v, axis=-1, keepdims=True)
        return (v - m) / jnp.sqrt(s + eps)

    def _to_tokens(v):
        B_, C_, H_, W_ = v.shape
        return v.reshape(B_, C_, H_ * W_).transpose(0, 2, 1)
    def _from_tokens(t, like):
        B_, C_, H_, W_ = like.shape
        return t.transpose(0, 2, 1).reshape(B_, C_, H_, W_)

    x = _L0_conv_ref(x, L0_conv_Wt, L0_conv_Wp, L0_conv_Wg, L0_conv_Wz, L0_conv_gn_w, L0_conv_gn_b)
    return x


_drawn_inputs = setup_inputs


def setup_inputs(seed=0):
    import zlib

    import numpy as np

    out = dict(_drawn_inputs(seed))
    spreads = {'L0_conv_gn_w': (1.0, 0.2), 'L0_conv_gn_b': (0.0, 0.1)}
    factors = {'L0_conv_Wt': 8.0, 'L0_conv_Wp': 8.0}
    for name, (base, spread) in spreads.items():
        noise = np.random.default_rng([zlib.crc32(name.encode()), seed]).standard_normal(out[name].shape)
        drawn = base * np.exp(spread * noise) if base else spread * noise
        out[name] = jnp.asarray(drawn.astype(out[name].dtype))
    for name, factor in factors.items():
        out[name] = (out[name] * factor).astype(out[name].dtype)
    return out
```

```python
import math
from contextlib import ExitStack

import concourse.bass as bass
from concourse import mybir

P = 128
NB, CIN, CP, HW = 16, 1024, 512, 1024
EPS = 1e-5
GAMMA = 1e-4
HALF = 512
NH = HW // HALF
KX = CIN // P
KY = CP // P
MZ = CIN // P
PAIRS = KX // 2
SLICE = 1024
SLICES = 8
SET = 4
NFIN = 4
ALPHA2 = [(2 * GAMMA) ** o / math.factorial(o) * math.exp(-2 * GAMMA) for o in range(3)]

FP32 = mybir.dt.float32
FP32R = mybir.dt.float32r
ALU = mybir.AluOpType
ACT = mybir.ActivationFunctionType
AX = mybir.AxisListType
RADD = bass.bass_isa.ReduceOp.add


def rbf_nonlocal_block(nc, x, wt_t, wp_t, wg_t, wz, wz_t, gn_w, gn_b, out):
    x_v = x.rearrange("b (k p) h w -> b p k (h w)", p=P)
    out_v = out.rearrange("b (m p) h w -> b p m (h w)", p=P)
    wt_v = wt_t.rearrange("(k p) o -> p k o", p=P)
    wp_v = wp_t.rearrange("(k p) o -> p k o", p=P)
    wg_v = wg_t.rearrange("(k p) o -> p k o", p=P)
    wz_v = wz.rearrange("(m p) c -> p m c", p=P)
    wzt_v = wz_t.rearrange("(k p) o -> p k o", p=P)

    ctx = ExitStack()
    with ctx:
        def sb(name, shape, dt=FP32):
            return ctx.enter_context(nc.sbuf_tensor(name, shape, dt))

        def sem(name):
            return ctx.enter_context(nc.semaphore(name))

        w_hi = sb("w_hi", [P, SLICES, SLICE], FP32R)
        w_lo = sb("w_lo", [P, SLICES, SLICE], FP32R)
        x_hi = sb("x_hi", [P, KX, HALF], FP32R)
        x_lo = sb("x_lo", [P, KX, HALF], FP32R)
        y_hi = sb("y_hi", [P, NH, KY, HALF], FP32R)
        y_lo = sb("y_lo", [P, NH, KY, HALF], FP32R)
        z_sb = sb("z_sb", [P, MZ, HW])
        x_raw = sb("x_raw", [P, PAIRS, 2, HALF])
        fin = sb("fin", [P, NFIN, HW])
        tmp_a = sb("tmp_a", [P, 2, HALF])
        tmp_b = sb("tmp_b", [P, 2, HALF])
        att_part = sb("att_part", [P, 3, NH * KY])
        att_sum = sb("att_sum", [P, NB, 3])
        alpha2 = sb("alpha2", [P, NB, 3])
        coef = sb("coef", [P, NB, 3])
        ones = sb("ones", [P, P])
        wz_rowsum = sb("wz_rowsum", [P, MZ])
        z_bias = sb("z_bias", [P, MZ])
        stats = sb("stats", [P, MZ * NH, 6])
        mean_var = sb("mean_var", [P, 2])
        st = sb("st", [P, 8])
        gnw = sb("gnw", [P, MZ])
        gnb = sb("gnb", [P, MZ])
        scale_a = sb("scale_a", [P, MZ])
        shift_b = sb("shift_b", [P, MZ])
        shift_t = sb("shift_t", [P, MZ])

        banks = [[ctx.enter_context(nc.psum_tensor(f"bank_{s}{i}", [P, HALF], FP32))
                  for i in range(SET)] for s in "ab"]
        SET_A, SET_B = banks

        w_landed = [sem(f"w_landed{s}") for s in range(SLICES)]
        x_landed = [sem(f"x_landed{q}") for q in range(PAIRS)]
        res_landed = [sem(f"res_landed{i}") for i in range(NFIN)]
        out_landed = [sem(f"out_landed{i}") for i in range(NFIN)]
        wz_landed = sem("wz_landed")
        gn_landed = sem("gn_landed")
        w_hi_ready = sem("w_hi_ready")
        w_lo_ready = sem("w_lo_ready")
        x_hi_ready = sem("x_hi_ready")
        x_lo_ready = sem("x_lo_ready")
        x_used = sem("x_used")
        consts_ready = sem("consts_ready")
        pg_done = sem("pg_done")
        g_copied = sem("g_copied")
        pg_ready = sem("pg_ready")
        pg_used = sem("pg_used")
        att_reduced = sem("att_reduced")
        att_done = sem("att_done")
        coef_ready = sem("coef_ready")
        rowsum_ready = sem("rowsum_ready")
        t_done = sem("t_done")
        u_ready = sem("u_ready")
        w_ready = sem("w_ready")
        y_hi_ready = sem("y_hi_ready")
        y_lo_ready = sem("y_lo_ready")
        z_done = sem("z_done")
        z_copied = sem("z_copied")
        z_bias_ready = sem("z_bias_ready")
        z_stat = sem("z_stat")
        mv_ready = sem("mv_ready")
        st_step = sem("st_step")
        ab_ready = sem("ab_ready")
        fin_scaled = sem("fin_scaled")
        fin_done = sem("fin_done")

        act_waited = sem("act_waited")
        dve_waited = sem("dve_waited")
        pool_waited = sem("pool_waited")

        block = ctx.enter_context(nc.Block())

        P2 = NB * NH
        G_STEPS = 8

        @block.sync
        def _(sp):
            def load_x(b, h, count):
                for q in range(PAIRS):
                    if not (isinstance(count, int) and count == 0):
                        sp.wait_ge(x_lo_ready, PAIRS * count - PAIRS + q + 1)
                    sp.dma_start(x_raw[:, q, :, :],
                                 x_v[b, :, 2 * q:2 * q + 2, h * HALF:(h + 1) * HALF]).then_inc(x_landed[q], 16)

            def load_res(b, m):
                slot = m % NFIN
                if not (isinstance(b, int) and b == 0 and m < NFIN):
                    sp.wait_ge(out_landed[slot], 16 * (b * (MZ // NFIN) + m // NFIN))
                sp.dma_start(fin[:, slot, :], x_v[b, :, m, :]).then_inc(res_landed[slot], 16)

            for s in range(SLICES):
                sp.dma_start(z_sb[:, s, 0:CP], wp_v[:, s, :]).then_inc(w_landed[s], 16)
                sp.dma_start(z_sb[:, s, CP:2 * CP], wg_v[:, s, :]).then_inc(w_landed[s], 16)
                if s % 2 == 0:
                    q = s // 2
                    sp.dma_start(x_raw[:, q, :, :], x_v[0, :, 2 * q:2 * q + 2, 0:HALF]).then_inc(x_landed[q], 16)
            sp.dma_start(gnw[:, :], gn_w).then_inc(gn_landed, 16)
            sp.dma_start(gnb[:, :], gn_b).then_inc(gn_landed, 16)
            load_x(0, 1, 1)
            sp.wait_ge(w_lo_ready, SLICES)
            sp.dma_start(z_sb[:, 0:KY, :].rearrange("p a (b c) -> p (a b) c", c=CP), wz_v).then_inc(wz_landed, 16)
            load_x(1, 0, 2)
            load_x(1, 1, 3)
            sp.wait_ge(rowsum_ready, 1)
            for s in range(SLICES):
                if s < KY:
                    src = wt_v[:, 2 * s:2 * s + 2, :]
                    sp.dma_start(z_sb[:, s, :].rearrange("p (k o) -> p k o", k=2), src).then_inc(w_landed[s], 16)
                else:
                    sp.dma_start(z_sb[:, s, :], wzt_v[:, s - KY, :]).then_inc(w_landed[s], 16)
            with sp.Fori(2, NB) as b:
                load_x(b, 0, 2 * b)
                load_x(b, 1, 2 * b + 1)

            load_x(0, 0, P2)
            load_x(0, 1, P2 + 1)
            for m in range(NFIN):
                load_res(0, m)
            load_x(1, 0, P2 + 2)
            load_x(1, 1, P2 + 3)
            with sp.Fori(1, NB - 1) as b:
                load_x(b + 1, 0, P2 + 2 * b + 2)
                for m in range(NFIN, MZ):
                    load_res(b - 1, m)
                load_x(b + 1, 1, P2 + 2 * b + 3)
                for m in range(NFIN):
                    load_res(b, m)
            for m in range(NFIN, MZ):
                load_res(NB - 2, m)
            for m in range(MZ):
                load_res(NB - 1, m)
            for slot in range(NFIN):
                sp.wait_ge(out_landed[slot], 16 * NB * (MZ // NFIN))

        @block.tensor
        def _(pe):
            def three_pass(bank, hi_w, lo_w, hi_x, lo_x, first, last):
                nc.tensor.matmul(bank, hi_w, hi_x, start=first, stop=False)
                nc.tensor.matmul(bank, hi_w, lo_x, start=False, stop=False)
                return nc.tensor.matmul(bank, lo_w, hi_x, start=False, stop=last)

            def pg_group(b, h, grp):
                group = 4 * b + 2 * h + grp
                for k in range(KX):
                    if isinstance(b, int) and b == 0 and h == 0 and grp == 0:
                        pe.wait_ge(w_lo_ready, k + 1)
                    if grp == 0 and k % 2 == 0:
                        pe.wait_ge(x_lo_ready, PAIRS * (2 * b + h) + k // 2 + 1)
                    for i in range(SET):
                        if k == 0 and i % 2 == 0 and not (isinstance(b, int) and b == 0 and h == 0):
                            pe.wait_ge(pg_used, 2 * (group - 2) + i // 2 + 1)
                        col = (i % 2) * CP + (2 * grp + i // 2) * P
                        mm = three_pass(banks[grp][i][:, :], w_hi[:, k, col:col + P], w_lo[:, k, col:col + P],
                                        x_hi[:, k, :], x_lo[:, k, :], k == 0, k == KX - 1)
                        if k == KX - 1:
                            mm.then_inc(pg_done, 1)
                    if grp == 1 and k % 2 == 1 and k < KX - 1:
                        mm.then_inc(x_used, 1)

            def pg_image(b):
                for h in range(NH):
                    for grp in range(2):
                        pg_group(b, h, grp)

            def t_group(b, h):
                half = 2 * b + h
                for k in range(KX):
                    if isinstance(b, int) and b == 0 and h == 0 and k % 2 == 0:
                        pe.wait_ge(w_lo_ready, SLICES + k // 2 + 1)
                    if k % 2 == 0:
                        pe.wait_ge(x_lo_ready, PAIRS * (P2 + half) + k // 2 + 1)
                    for i in range(SET):
                        if k == 0 and isinstance(b, int) and b == 0:
                            if i % 2 == 0:
                                pe.wait_ge(pg_used, 2 * (4 * NB - 2 + h) + i // 2 + 1)
                            if h == 1 and i == 0:
                                pe.wait_ge(coef_ready, 1)
                        elif k == 0:
                            pe.wait_ge(z_copied, 16 * (b - 1) + 8 * h + i + 1)
                        col = (k % 2) * CP + i * P
                        mm = three_pass(banks[h][i][:, :], w_hi[:, k // 2, col:col + P],
                                        w_lo[:, k // 2, col:col + P],
                                        x_hi[:, k, :], x_lo[:, k, :], k == 0, k == KX - 1)
                        if k == KX - 1:
                            mm.then_inc(t_done, 1)
                    if k % 2 == 1 and k < KX - 1:
                        mm.then_inc(x_used, 1)
                    if isinstance(b, int) and b == 0 and h == 0 and k == KX // 2:
                        pe.wait_ge(consts_ready, 1)
                        pe.wait_ge(att_reduced, NB)
                        nc.tensor.matmul(SET_B[0][:, 0:3 * NB], ones[:, :],
                                         att_sum[:, :, :].rearrange("p b j -> p (b j)"),
                                         start=True, stop=True).then_inc(att_done, 1)

            def z_group(b, h, grp, last=False):
                use = banks[(h + grp) % 2]
                for k in range(KY):
                    if grp == 0:
                        pe.wait_ge(y_lo_ready, KY * (2 * b + h) + k + 1)
                    for i in range(SET):
                        if k == 0:
                            if h == 0 and grp == 0:
                                if isinstance(b, int) and b == 0:
                                    pe.wait_ge(t_used_sem, i + 1)
                                else:
                                    pe.wait_ge(z_copied, 16 * (b - 1) + 12 + i + 1)
                            elif h == 0:
                                pe.wait_ge(t_used_sem, 4 * (2 * b + 1) + i + 1)
                            elif grp == 0:
                                pe.wait_ge(z_copied, 16 * b + 4 + i + 1)
                            elif last:
                                pe.wait_ge(z_copied, 16 * b + i + 1)
                            else:
                                pe.wait_ge(t_used_sem, 4 * (2 * b + 2) + i + 1)
                            if isinstance(b, int) and b == 0 and h == 0 and grp == 0 and i == 0:
                                pe.wait_ge(w_lo_ready, 2 * SLICES)
                        col = (4 * grp + i) * P
                        mm = three_pass(use[i][:, :], w_hi[:, KY + k, col:col + P], w_lo[:, KY + k, col:col + P],
                                        y_hi[:, h, k, :], y_lo[:, h, k, :], k == 0, k == KY - 1)
                        if k == KY - 1:
                            mm.then_inc(z_done, 1)

            t_used_sem = w_ready

            pg_image(0)
            with pe.Fori(1, NB) as b:
                pg_image(b)

            def body(b, last=False):
                t_group(b, 1)
                z_group(b, 0, 0)
                z_group(b, 0, 1)
                if not last:
                    t_group(b + 1, 0)
                z_group(b, 1, 0)
                z_group(b, 1, 1, last)

            t_group(0, 0)
            body(0)
            with pe.Fori(1, NB - 1) as b:
                body(b)
            body(NB - 1, last=True)

        @block.scalar
        def _(act):
            def split_w(s, phase):
                act.wait_ge(w_landed[s], 32 if phase == 0 else 48)
                if phase == 1 and s >= KY:
                    act.wait_ge(pg_done, 16 * NB)
                nc.scalar.copy(w_hi[:, s, :], z_sb[:, s, :]).then_inc(w_hi_ready, 1)

            def split_x(q, count, phase):
                act.wait_ge(x_landed[q], 16 * count + 16)
                if isinstance(count, int) and count == 0:
                    pass
                elif q < PAIRS - 1:
                    act.wait_ge(x_used, (PAIRS - 1) * (count - 1) + q + 1)
                elif phase == 0:
                    act.wait_ge(pg_done, 2 * KY * count)
                else:
                    act.wait_ge(t_done, KY * (count - P2))
                nc.scalar.copy(x_hi[:, 2 * q:2 * q + 2, :], x_raw[:, q, :, :]).then_inc(x_hi_ready, 1)

            def copy_g(b, h, grp):
                for j in range(2):
                    n = 8 * b + 4 * h + 2 * grp + j
                    act.wait_ge(pg_done, 2 * n + 2)
                    if not (isinstance(b, int) and b == 0 and h == 0 and grp == 0):
                        act.wait_ge(pg_ready, n - 1)
                    if not (isinstance(b, int) and b == 0) and h == 0 and grp == 0 and j == 0:
                        act.wait_ge(att_reduced, b)
                    i = KY * h + 2 * grp + j
                    nc.scalar.activation(tmp_a[:, j, :], banks[grp][2 * j + 1][:, :], ACT.Identity,
                                         accum_out=att_part[:, 0, i:i + 1]).then_inc(g_copied, 1)

            def pg_image(b, last=False):
                for h in range(NH):
                    copy_g(b, h, 0)
                    for q in range(PAIRS):
                        split_x(q, 2 * b + h + 1, 0)
                        if last and h == NH - 1:
                            split_w(q, 1)
                    copy_g(b, h, 1)

            def t_to_y(b, h):
                def u(i):
                    n = 4 * (2 * b + h) + i
                    act.wait_ge(t_done, n + 1)
                    if not (isinstance(b, int) and b == 0 and h == 0 and i < 2):
                        act.wait_ge(w_ready, n - 1)
                    else:
                        act.wait_ge(pg_ready, 8 * NB)
                        act.wait_ge(coef_ready, 1)
                    act.sem_inc(act_waited, 1)
                    nc.scalar.activation(tmp_a[:, i % 2, :], banks[h][i][:, :], ACT.Identity,
                                         bias=coef[:, b, 1:2], scale=coef[:, b, 2:3]).then_inc(u_ready, 1)

                def hi(i):
                    n = 4 * (2 * b + h) + i
                    act.wait_ge(w_ready, n + 1)
                    if not (isinstance(b, int) and b == 0):
                        act.wait_ge(z_done, 16 * (b - 1) + 8 * h + 8)
                    nc.scalar.copy(y_hi[:, h, i, :], tmp_b[:, i % 2, :]).then_inc(y_hi_ready, 1)

                u(0)
                u(1)
                hi(0)
                u(2)
                hi(1)
                u(3)
                hi(2)
                hi(3)

            def copy_z(b, h, grp):
                for i in range(SET):
                    m = 4 * grp + i
                    act.wait_ge(z_done, 16 * b + 8 * h + m + 1)
                    if h == 0 and m == 0:
                        act.wait_ge(z_bias_ready, b + 1)
                    if h == 0 and not (isinstance(b, int) and b == 0):
                        act.wait_ge(fin_scaled, MZ * (b - 1) + m + 1)
                    nc.scalar.activation(z_sb[:, m, h * HALF:(h + 1) * HALF], banks[(h + grp) % 2][i][:, :],
                                         ACT.Identity, bias=z_bias[:, m:m + 1]).then_inc(z_copied, 1)

            def finish(b, m0, m1):
                for m in range(m0, m1):
                    act.wait_ge(fin_scaled, MZ * b + m + 1)
                    nc.scalar.activation(fin[:, m % NFIN, :], fin[:, m % NFIN, :], ACT.Identity,
                                         bias=shift_b[:, m:m + 1]).then_inc(fin_done, 1)
                    act.wait_ge(fin_done, MZ * b + m + 1)
                    act.dma_start(out_v[b, :, m, :], fin[:, m % NFIN, :]).then_inc(out_landed[m % NFIN], 16)

            for s in range(SLICES):
                split_w(s, 0)
                if s % 2 == 0:
                    split_x(s // 2, 0, 0)
            pg_image(0)
            with act.Fori(1, NB - 1) as b:
                pg_image(b)
            pg_image(NB - 1, last=True)

            def body(b, last=False):
                if not (isinstance(b, int) and b == 0):
                    copy_z(b - 1, 1, 1)
                    finish(b - 1, 0, NFIN)
                t_to_y(b, 1)
                if not last:
                    for q in range(PAIRS):
                        split_x(q, P2 + 2 * b + 2, 1)
                if not (isinstance(b, int) and b == 0):
                    finish(b - 1, NFIN, MZ)
                copy_z(b, 0, 0)
                copy_z(b, 0, 1)
                if not last:
                    t_to_y(b + 1, 0)
                    for q in range(PAIRS):
                        split_x(q, P2 + 2 * b + 3, 1)
                copy_z(b, 1, 0)

            for s in range(KY, SLICES):
                split_w(s, 1)
            for q in range(PAIRS):
                split_x(q, P2 + 1, 1)
            t_to_y(0, 0)
            body(0)
            with act.Fori(1, NB - 1) as b:
                body(b)
            body(NB - 1, last=True)
            copy_z(NB - 1, 1, 1)
            finish(NB - 1, 0, MZ)

        @block.vector
        def _(dve):
            def split_w(s, phase):
                dve.wait_ge(w_hi_ready, SLICES * phase + s + 1)
                nc.vector.tensor_tensor(w_lo[:, s, :], z_sb[:, s, :], w_hi[:, s, :].bitcast(FP32),
                                        ALU.subtract).then_inc(w_lo_ready, 1)

            def split_x(q, count):
                dve.wait_ge(x_hi_ready, PAIRS * count + q + 1)
                nc.vector.tensor_tensor(x_lo[:, 2 * q:2 * q + 2, :], x_raw[:, q, :, :],
                                        x_hi[:, 2 * q:2 * q + 2, :].bitcast(FP32),
                                        ALU.subtract).then_inc(x_lo_ready, 1)

            def sum_pg(b, h, grp):
                for j in range(2):
                    n = 8 * b + 4 * h + 2 * grp + j
                    i = KY * h + 2 * grp + j
                    dve.wait_ge(g_copied, n + 1)
                    if not (isinstance(b, int) and b == 0 and h == 0 and grp == 0):
                        dve.wait_ge(pg_used, n - 1)
                    nc.vector.scalar_tensor_tensor(out=tmp_b[:, j, :], in0=banks[grp][2 * j][:, :], scalar=1.0,
                                                   in1=tmp_a[:, j, :], op0=ALU.mult, op1=ALU.mult,
                                                   accum_out=att_part[:, 1, i:i + 1]).then_inc(pg_ready, 1)
                for j in range(2):
                    n = 8 * b + 4 * h + 2 * grp + j
                    i = KY * h + 2 * grp + j
                    dve.wait_ge(pg_ready, n + 1)
                    nc.vector.scalar_tensor_tensor(out=tmp_b[:, j, :], in0=banks[grp][2 * j][:, :], scalar=1.0,
                                                   in1=tmp_b[:, j, :], op0=ALU.mult, op1=ALU.mult,
                                                   accum_out=att_part[:, 2, i:i + 1]).then_inc(pg_used, 1)

            def pg_image(b, last=False):
                for h in range(NH):
                    sum_pg(b, h, 0)
                    for q in range(PAIRS):
                        split_x(q, 2 * b + h + 1)
                        if last and h == NH - 1:
                            split_w(q, 1)
                    sum_pg(b, h, 1)
                dve.wait_ge(pg_used, 8 * b + 8)
                nc.vector.tensor_reduce(att_sum[:, b, :], att_part[:, :, :], AX.X, ALU.add).then_inc(att_reduced, 1)

            def t_to_y(b, h):
                def w(i):
                    n = 4 * (2 * b + h) + i
                    dve.wait_ge(u_ready, n + 1)
                    if not (isinstance(b, int) and b == 0 and h == 0 and i < 2):
                        dve.wait_ge(y_lo_ready, n - 1)
                    nc.vector.tensor_tensor(tmp_b[:, i % 2, :], banks[h][i][:, :], tmp_a[:, i % 2, :],
                                            ALU.mult).then_inc(w_ready, 1)

                def lo(i):
                    n = 4 * (2 * b + h) + i
                    dve.wait_ge(y_hi_ready, n + 1)
                    nc.vector.tensor_tensor(y_lo[:, h, i, :], tmp_b[:, i % 2, :], y_hi[:, h, i, :].bitcast(FP32),
                                            ALU.subtract).then_inc(y_lo_ready, 1)

                w(0)
                w(1)
                lo(0)
                w(2)
                lo(1)
                w(3)
                lo(2)
                lo(3)

            def z_stats(b, h, grp):
                for i in range(SET):
                    m = 4 * grp + i
                    dve.wait_ge(z_copied, 16 * b + 8 * h + m + 1)
                    if h == 0 and m == 0 and not (isinstance(b, int) and b == 0):
                        dve.wait_ge(mv_ready, b)
                    nc.vector.bn_stats(stats[:, 8 * h + m, :],
                                       z_sb[:, m, h * HALF:(h + 1) * HALF]).then_inc(z_stat, 1)

            def image_stats(b):
                dve.wait_ge(z_stat, 16 * b + 16)
                if not (isinstance(b, int) and b == 0):
                    dve.wait_ge(ab_ready, b)
                dve.sem_inc(dve_waited, 1)
                nc.vector.bn_aggr(mean_var[:, :], stats[:, :, :].rearrange("p a b -> p (a b)")).then_inc(mv_ready, 1)

            def bias(b):
                if not (isinstance(b, int) and b == 0):
                    dve.wait_ge(z_copied, 16 * b)
                nc.vector.tensor_scalar(z_bias[:, :], wz_rowsum[:, :], coef[:, b, 0:1], None,
                                        ALU.mult).then_inc(z_bias_ready, 1)

            def scale(b, m0, m1):
                for m in range(m0, m1):
                    if m == m0:
                        dve.wait_ge(ab_ready, b + 1)
                    dve.wait_ge(res_landed[m % NFIN], 16 * (b * (MZ // NFIN) + m // NFIN) + 16)
                    nc.vector.scalar_tensor_tensor(out=fin[:, m % NFIN, :], in0=z_sb[:, m, :],
                                                   scalar=scale_a[:, m:m + 1], in1=fin[:, m % NFIN, :],
                                                   op0=ALU.mult, op1=ALU.add).then_inc(fin_scaled, 1)

            for s in range(SLICES):
                split_w(s, 0)
                if s % 2 == 0:
                    split_x(s // 2, 0)
            pg_image(0)
            dve.wait_ge(wz_landed, 16)
            nc.vector.tensor_reduce(wz_rowsum[:, :],
                                    z_sb[:, 0:KY, :].rearrange("p a (b c) -> p (a b) c", c=CP), AX.X,
                                    ALU.add).then_inc(rowsum_ready, 1)
            with dve.Fori(1, NB - 1) as b:
                pg_image(b)
            pg_image(NB - 1, last=True)

            def body(b, last=False):
                if not (isinstance(b, int) and b == 0):
                    z_stats(b - 1, 1, 1)
                    image_stats(b - 1)
                bias(b)
                if not (isinstance(b, int) and b == 0):
                    scale(b - 1, 0, NFIN)
                t_to_y(b, 1)
                if not last:
                    for q in range(PAIRS):
                        split_x(q, P2 + 2 * b + 2)
                if not (isinstance(b, int) and b == 0):
                    scale(b - 1, NFIN, MZ)
                z_stats(b, 0, 0)
                z_stats(b, 0, 1)
                if not last:
                    t_to_y(b + 1, 0)
                    for q in range(PAIRS):
                        split_x(q, P2 + 2 * b + 3)
                z_stats(b, 1, 0)

            for s in range(KY, SLICES):
                split_w(s, 1)
            for q in range(PAIRS):
                split_x(q, P2 + 1)
            dve.wait_ge(att_done, 1)
            nc.vector.tensor_tensor(coef[:, :, :].rearrange("p b j -> p (b j)"), SET_B[0][:, 0:3 * NB],
                                    alpha2[:, :, :].rearrange("p b j -> p (b j)"),
                                    ALU.mult).then_inc(coef_ready, 1)
            dve.wait_ge(coef_ready, 1)
            dve.wait_ge(rowsum_ready, 1)
            t_to_y(0, 0)
            body(0)
            with dve.Fori(1, NB - 1) as b:
                body(b)
            body(NB - 1, last=True)
            z_stats(NB - 1, 1, 1)
            image_stats(NB - 1)
            scale(NB - 1, 0, MZ)

        @block.gpsimd
        def _(pool):
            for j in range(3):
                nc.gpsimd.memset(alpha2[:, :, j:j + 1], ALPHA2[j])
            nc.gpsimd.memset(st[:, 7:8], -0.5)
            nc.gpsimd.memset(ones[:, :], 1.0).then_inc(consts_ready, 1)
            pool.wait_ge(consts_ready, 1)
            pool.wait_ge(gn_landed, 32)

            def channel_factors(b):
                def step(ins, n):
                    ins.then_inc(st_step, 1)
                    pool.wait_ge(st_step, G_STEPS * b + n)
                    pool.sem_inc(pool_waited, 1)

                pool.wait_ge(mv_ready, b + 1)
                pool.sem_inc(pool_waited, 1)
                step(nc.gpsimd.partition_all_reduce(st[:, 0:1], mean_var[:, 0:1], P, RADD), 1)
                step(nc.gpsimd.tensor_scalar(st[:, 1:2], st[:, 0:1], -1.0 / P, 0.0, ALU.mult, ALU.add), 2)
                step(nc.gpsimd.tensor_tensor(st[:, 2:3], mean_var[:, 0:1], st[:, 1:2], ALU.add), 3)
                step(nc.gpsimd.tensor_scalar(st[:, 3:4], st[:, 2:3], st[:, 2:3], mean_var[:, 1:2],
                                             ALU.mult, ALU.add), 4)
                step(nc.gpsimd.partition_all_reduce(st[:, 4:5], st[:, 3:4], P, RADD), 5)
                step(nc.gpsimd.tensor_scalar(st[:, 5:6], st[:, 4:5], 1.0 / P, EPS, ALU.mult, ALU.add), 6)
                step(nc.gpsimd.tensor_tensor(st[:, 6:7], st[:, 5:6], st[:, 7:8], ALU.pow), 7)
                if not (isinstance(b, int) and b == 0):
                    pool.wait_ge(fin_done, MZ * b)
                    pool.sem_inc(pool_waited, 1)
                nc.gpsimd.tensor_scalar(scale_a[:, :], gnw[:, :], st[:, 6:7], 1.0, ALU.mult, ALU.mult)
                step(nc.gpsimd.tensor_scalar(shift_t[:, :], gnw[:, :], st[:, 6:7], st[:, 1:2],
                                             ALU.mult, ALU.mult), 8)
                nc.gpsimd.tensor_tensor(shift_b[:, :], shift_t[:, :], gnb[:, :], ALU.add).then_inc(ab_ready, 1)

            channel_factors(0)
            with pool.Fori(1, NB) as b:
                channel_factors(b)


_OUT_SHAPE = (NB, CIN, 32, 32)


def kernel(x, L0_conv_Wt, L0_conv_Wp, L0_conv_Wg, L0_conv_Wz, L0_conv_gn_w, L0_conv_gn_b):
    import numpy as _np
    import concourse.bacc as _bacc
    from concourse import mybir as _mybir
    from concourse.bass_utils import run_bass_kernel_spmd as _run

    nc = _bacc.Bacc("TRN2", target_bir_lowering=False, num_devices=1)
    given = {
        "x": x,
        "wt_t": _np.transpose(L0_conv_Wt),
        "wp_t": _np.transpose(L0_conv_Wp),
        "wg_t": _np.transpose(L0_conv_Wg),
        "wz": L0_conv_Wz,
        "wz_t": _np.transpose(L0_conv_Wz),
        "gn_w": _np.transpose(_np.reshape(L0_conv_gn_w, (MZ, P))),
        "gn_b": _np.transpose(_np.reshape(L0_conv_gn_b, (MZ, P))),
    }
    arrays = {f"in_{name}_dram": _np.ascontiguousarray(a) for name, a in given.items()}
    args = [nc.dram_tensor(name, a.shape, _mybir.dt.from_np(a.dtype), kind="ExternalInput").ap()
            for name, a in arrays.items()]
    out = nc.dram_tensor("out_0_dram", _OUT_SHAPE, FP32, kind="ExternalOutput").ap()
    rbf_nonlocal_block(nc, *args, out)
    r = _run(nc, [arrays], core_ids=[0])
    return r.results[0]["out_0_dram"]
```

```python
import math
from contextlib import ExitStack

import concourse.bass as bass
from concourse import mybir

P = 128
NB, CIN, CP, HW = 16, 1024, 512, 1024
EPS = 1e-5
GAMMA = 1e-4
HALF = 512
NH = HW // HALF
KX = CIN // P
KY = CP // P
MZ = CIN // P
PAIRS = KX // 2
SLICE = 1024
SLICES = 8
SET = 4
NFIN = 4

STAGES = 7
KB = KX // 2
R11, R12, R21, R22, RT = range(5)
B_FROM = (R11, RT, R21, R12, R11, RT, R22)
A_ORDER = (0, 5, 1, 2, 6, 3, 4)
OPENS = (0, 1, 4)
P1_COPY, P6_SUM, C11, P67_SUM, C22, C21, C12 = range(7)
READS = 20
READ_AT = {P6_SUM: 0, P67_SUM: 4, C22: 8, C21: 12, C12: 16}
PAIR_AT = {C11: 0, C22: 2, C21: 4, C12: 6}
ALPHA2 = [(2 * GAMMA) ** o / math.factorial(o) * math.exp(-2 * GAMMA) for o in range(3)]

FP32 = mybir.dt.float32
FP32R = mybir.dt.float32r
ALU = mybir.AluOpType
ACT = mybir.ActivationFunctionType
AX = mybir.AxisListType
RADD = bass.bass_isa.ReduceOp.add


def rbf_nonlocal_block(nc, x, wt_t, wpg_t, wz, wz_t, gn_w, gn_b, out):
    x_v = x.rearrange("b (k p) h w -> b p k (h w)", p=P)
    out_v = out.rearrange("b (m p) h w -> b p m (h w)", p=P)
    wt_v = wt_t.rearrange("(k p) o -> p k o", p=P)
    wpg_v = wpg_t.rearrange("(k p) u o -> p k u o", p=P)
    wz_v = wz.rearrange("(m p) c -> p m c", p=P)
    wzt_v = wz_t.rearrange("(k p) o -> p k o", p=P)

    ctx = ExitStack()
    with ctx:
        def sb(name, shape, dt=FP32):
            return ctx.enter_context(nc.sbuf_tensor(name, shape, dt))

        def sem(name):
            return ctx.enter_context(nc.semaphore(name))

        split_t = sb("split_t", [P, 64, HALF], FP32R)
        flat_t = sb("flat_t", [P, 36, HALF])
        sum67, p1_buf, sum6 = flat_t[:, 20:24, :], flat_t[:, 24:28, :], flat_t[:, 28:32, :]
        a21_raw, a11_raw, a12_raw, a22_raw = (flat_t[:, i:i + 4, :] for i in (20, 24, 28, 32))
        z_sb = flat_t[:, 0:16, :].rearrange("p (m h) n -> p m (h n)", h=NH)
        x_raw = flat_t[:, 16:24, :].rearrange("p (q c) n -> p q c n", c=2)
        fin = flat_t[:, 24:32, :].rearrange("p (i h) n -> p i (h n)", h=NH)
        tmp_a, tmp_b = flat_t[:, 32:34, :], flat_t[:, 34:36, :]
        w_hi = split_t[:, 0:16, :].rearrange("p (s c) n -> p s (c n)", c=2)
        w_lo = split_t[:, 16:32, :].rearrange("p (s c) n -> p s (c n)", c=2)
        x_hi, x_lo = split_t[:, 32:40, :], split_t[:, 40:48, :]
        y_hi = split_t[:, 48:56, :].rearrange("p (h k) n -> p h k n", h=NH)
        y_lo = split_t[:, 56:64, :].rearrange("p (h k) n -> p h k n", h=NH)
        b_hi, b_lo = split_t[:, 56:60, :], split_t[:, 60:64, :]
        att_part = sb("att_part", [P, 3, NH * KY])
        att_sum = sb("att_sum", [P, NB, 3])
        alpha2 = sb("alpha2", [P, NB, 3])
        coef = sb("coef", [P, NB, 3])
        ones = sb("ones", [P, P])
        wz_rowsum = sb("wz_rowsum", [P, MZ])
        z_bias = sb("z_bias", [P, MZ])
        stats = sb("stats", [P, MZ * NH, 6])
        mean_var = sb("mean_var", [P, 2])
        st = sb("st", [P, 8])
        gnw = sb("gnw", [P, MZ])
        gnb = sb("gnb", [P, MZ])
        scale_a = sb("scale_a", [P, MZ])
        shift_b = sb("shift_b", [P, MZ])
        shift_t = sb("shift_t", [P, MZ])

        banks = [[ctx.enter_context(nc.psum_tensor(f"bank_{s}{i}", [P, HALF], FP32))
                  for i in range(SET)] for s in "ab"]
        SET_A, SET_B = banks

        a_landed = [sem(f"a_landed{i}") for i in range(4)]
        b_landed = [sem(f"b_landed{i}") for i in range(4)]
        b_first = [sem(f"b_first{k}") for k in range(KB)]
        w_landed = [sem(f"w_landed{s}") for s in range(SLICES)]
        x_landed = [sem(f"x_landed{q}") for q in range(PAIRS)]
        res_landed = [sem(f"res_landed{i}") for i in range(NFIN)]
        out_landed = [sem(f"out_landed{i}") for i in range(NFIN)]
        wz_landed = sem("wz_landed")
        gn_landed = sem("gn_landed")
        a_hi_ready = sem("a_hi_ready")
        a_lo_ready = sem("a_lo_ready")
        a_summed = sem("a_summed")
        b_hi_ready = sem("b_hi_ready")
        b_lo_ready = sem("b_lo_ready")
        b_summed = sem("b_summed")
        b_used = sem("b_used")
        prod_done = sem("prod_done")
        p1_copied = sem("p1_copied")
        bank_read = sem("bank_read")
        g_copied = sem("g_copied")
        pg_ready = sem("pg_ready")
        pair_summed = sem("pair_summed")
        att_reduced = sem("att_reduced")
        att_done = sem("att_done")
        coef_ready = sem("coef_ready")
        rowsum_ready = sem("rowsum_ready")
        consts_ready = sem("consts_ready")
        w_hi_ready = sem("w_hi_ready")
        w_lo_ready = sem("w_lo_ready")
        x_hi_ready = sem("x_hi_ready")
        x_lo_ready = sem("x_lo_ready")
        x_used = sem("x_used")
        t_done = sem("t_done")
        u_ready = sem("u_ready")
        w_ready = sem("w_ready")
        y_hi_ready = sem("y_hi_ready")
        y_lo_ready = sem("y_lo_ready")
        z_done = sem("z_done")
        z_copied = sem("z_copied")
        z_bias_ready = sem("z_bias_ready")
        z_stat = sem("z_stat")
        mv_ready = sem("mv_ready")
        st_step = sem("st_step")
        ab_ready = sem("ab_ready")
        fin_scaled = sem("fin_scaled")
        fin_done = sem("fin_done")

        act_waited = sem("act_waited")
        dve_waited = sem("dve_waited")
        pool_waited = sem("pool_waited")
        sp_waited = sem("sp_waited")

        block = ctx.enter_context(nc.Block())

        LAST = NB - 1
        G_STEPS = 8

        @block.sync
        def _(sp):
            def load_b(b):
                done = 4 * STAGES * (b - 1)
                sp.wait_ge(b_summed, 8 * (b - 1) + 8)
                sp.wait_ge(b_lo_ready, done + 4 * 2 + 4)
                sp.sem_inc(sp_waited, 1)
                sp.dma_start(flat_t[:, 4 * R21:4 * R21 + 4, :], x_v[b, :, KB:KX, 0:HALF]).then_inc(b_landed[R21], 16)
                sp.wait_ge(b_lo_ready, done + 4 * 3 + 4)
                sp.sem_inc(sp_waited, 1)
                sp.dma_start(flat_t[:, 4 * R12:4 * R12 + 4, :], x_v[b, :, 0:KB, HALF:HW]).then_inc(b_landed[R12], 16)
                sp.wait_ge(b_lo_ready, done + 4 * 4 + 4)
                sp.sem_inc(sp_waited, 1)
                sp.dma_start(flat_t[:, 4 * R11:4 * R11 + 4, :], x_v[b, :, 0:KB, 0:HALF]).then_inc(b_landed[R11], 16)
                sp.wait_ge(b_lo_ready, done + 4 * 6 + 4)
                sp.sem_inc(sp_waited, 1)
                sp.dma_start(flat_t[:, 4 * R22:4 * R22 + 4, :], x_v[b, :, KB:KX, HALF:HW]).then_inc(b_landed[R22], 16)

            def load_x(b, h, first=False):
                for q in range(PAIRS):
                    if not first:
                        sp.wait_ge(x_lo_ready, PAIRS * (2 * b + h - 1) + q + 1)
                    sp.dma_start(x_raw[:, q, :, :],
                                 x_v[b, :, 2 * q:2 * q + 2, h * HALF:(h + 1) * HALF]).then_inc(x_landed[q], 16)

            def load_res(b, m):
                slot = m % NFIN
                if not (isinstance(b, int) and b == 0 and m < NFIN):
                    sp.wait_ge(out_landed[slot], 16 * (b * (MZ // NFIN) + m // NFIN))
                sp.dma_start(fin[:, slot, :], x_v[b, :, m, :]).then_inc(res_landed[slot], 16)

            for k in range(KB):
                sp.dma_start(a11_raw[:, k, :], wpg_v[:, k, 0, :]).then_inc(a_landed[0], 16)
                sp.dma_start(flat_t[:, 4 * R11 + k, :], x_v[0, :, k, 0:HALF]).then_inc(b_first[k], 16)
            sp.dma_start(a22_raw, wpg_v[:, KB:KX, 1, :]).then_inc(a_landed[1], 16)
            sp.dma_start(a21_raw, wpg_v[:, 0:KB, 1, :]).then_inc(a_landed[2], 16)
            sp.dma_start(flat_t[:, 4 * R12:4 * R12 + 4, :], x_v[0, :, 0:KB, HALF:HW]).then_inc(b_landed[R12], 16)
            sp.dma_start(flat_t[:, 4 * R22:4 * R22 + 4, :], x_v[0, :, KB:KX, HALF:HW]).then_inc(b_landed[R22], 16)
            sp.dma_start(a12_raw, wpg_v[:, KB:KX, 0, :]).then_inc(a_landed[3], 16)
            sp.dma_start(flat_t[:, 4 * R21:4 * R21 + 4, :], x_v[0, :, KB:KX, 0:HALF]).then_inc(b_landed[R21], 16)
            sp.dma_start(gnw[:, :], gn_w).then_inc(gn_landed, 16)
            sp.dma_start(gnb[:, :], gn_b).then_inc(gn_landed, 16)
            with sp.Fori(1, NB) as b:
                load_b(b)

            done = 4 * STAGES * LAST
            sp.wait_ge(b_lo_ready, done + 4 * 3 + 4)
            for s in (2, 3):
                sp.dma_start(z_sb[:, s, :].rearrange("p (k o) -> p k o", k=2),
                             wt_v[:, 2 * s:2 * s + 2, :]).then_inc(w_landed[s], 16)
            sp.wait_ge(b_lo_ready, done + 4 * 4 + 4)
            for s in (0, 1):
                sp.dma_start(z_sb[:, s, :].rearrange("p (k o) -> p k o", k=2),
                             wt_v[:, 2 * s:2 * s + 2, :]).then_inc(w_landed[s], 16)
            sp.wait_ge(b_summed, 8 * LAST + 8)
            for s in (4, 5):
                sp.dma_start(z_sb[:, s, :], wzt_v[:, s - KY, :]).then_inc(w_landed[s], 16)
            sp.wait_ge(b_lo_ready, done + 4 * 5 + 4)
            sp.wait_ge(pair_summed, 8 * LAST + 4)
            load_x(0, 0, True)
            sp.wait_ge(b_lo_ready, done + 4 * 6 + 4)
            for s in (6, 7):
                sp.dma_start(z_sb[:, s, :], wzt_v[:, s - KY, :]).then_inc(w_landed[s], 16)
            sp.wait_ge(att_reduced, NB)
            sp.dma_start(fin.rearrange("p a (b c) -> p (a b) c", c=CP), wz_v).then_inc(wz_landed, 16)

            load_x(0, 1)
            sp.wait_ge(rowsum_ready, 1)
            for m in range(NFIN):
                load_res(0, m)
            load_x(1, 0)
            load_x(1, 1)
            with sp.Fori(1, NB - 1) as b:
                load_x(b + 1, 0)
                for m in range(NFIN, MZ):
                    load_res(b - 1, m)
                load_x(b + 1, 1)
                for m in range(NFIN):
                    load_res(b, m)
            for m in range(NFIN, MZ):
                load_res(NB - 2, m)
            for m in range(MZ):
                load_res(NB - 1, m)
            for slot in range(NFIN):
                sp.wait_ge(out_landed[slot], 16 * NB * (MZ // NFIN))

        @block.tensor
        def _(pe):
            def three_pass(bank, hi_w, lo_w, hi_x, lo_x, first, last, resumed=False):
                nc.tensor.matmul(bank, hi_w, hi_x, start=first, stop=False, skip_group_check=resumed)
                nc.tensor.matmul(bank, hi_w, lo_x, start=False, stop=False, skip_group_check=resumed)
                return nc.tensor.matmul(bank, lo_w, hi_x, start=False, stop=last, skip_group_check=resumed)

            def stage(b, j, odd):
                use = banks[(j + odd) % 2]
                count = STAGES * b + j
                for k in range(KB):
                    if isinstance(b, int) and b == 0:
                        pe.wait_ge(a_lo_ready, KB * A_ORDER.index(j) + k + 1)
                    pe.wait_ge(b_lo_ready, KB * count + k + 1)
                    for i in range(SET):
                        if k == 0 and j == 0 and not (isinstance(b, int) and b == 0):
                            pe.wait_ge(bank_read, READS * (b - 1) + READ_AT[C21] + i + 1)
                        elif k == 0 and j == 1 and not (isinstance(b, int) and b == 0):
                            pe.wait_ge(bank_read, READS * (b - 1) + READ_AT[C12] + i + 1)
                        elif k == 0 and j == 2:
                            pe.wait_ge(p1_copied, SET * b + i + 1)
                        elif k == 0 and j == 3:
                            pe.wait_ge(bank_read, READS * b + READ_AT[P6_SUM] + i + 1)
                        elif k == 0 and j == 4 and i % 2 == 0:
                            pe.wait_ge(pair_summed, 8 * b + PAIR_AT[C11] + i // 2 + 1)
                        elif k == 0 and j == 5:
                            pe.wait_ge(bank_read, READS * b + READ_AT[P67_SUM] + i + 1)
                        elif k == 0 and j == 6:
                            pe.wait_ge(bank_read, READS * b + READ_AT[C22] + i + 1)
                        hi_a = split_t[:, 8 * j + k, i * P:(i + 1) * P]
                        lo_a = split_t[:, 8 * j + KB + k, i * P:(i + 1) * P]
                        mm = three_pass(use[i][:, :], hi_a, lo_a, b_hi[:, k, :], b_lo[:, k, :],
                                        k == 0 and j in OPENS, k == KB - 1, j not in OPENS)
                        if k == KB - 1:
                            mm.then_inc(prod_done, 1)
                    if k < KB - 1:
                        mm.then_inc(b_used, 1)

            def pg_image(b, odd):
                for j in range(STAGES):
                    stage(b, j, odd)

            def t_group(b, h):
                half = 2 * b + h
                for k in range(KX):
                    if isinstance(b, int) and b == 0 and h == 0 and k % 2 == 0:
                        pe.wait_ge(w_lo_ready, k // 2 + 1)
                    if k % 2 == 0:
                        pe.wait_ge(x_lo_ready, PAIRS * half + k // 2 + 1)
                    for i in range(SET):
                        if k == 0 and isinstance(b, int) and b == 0:
                            pe.wait_ge(bank_read, READS * LAST + READ_AT[(C21, C12)[h]] + i + 1)
                            if h == 1 and i == 0:
                                pe.wait_ge(coef_ready, 1)
                        elif k == 0:
                            pe.wait_ge(z_copied, 16 * (b - 1) + 8 * h + i + 1)
                        col = (k % 2) * CP + i * P
                        mm = three_pass(banks[h][i][:, :], w_hi[:, k // 2, col:col + P],
                                        w_lo[:, k // 2, col:col + P],
                                        x_hi[:, k, :], x_lo[:, k, :], k == 0, k == KX - 1)
                        if k == KX - 1:
                            mm.then_inc(t_done, 1)
                    if k % 2 == 1 and k < KX - 1:
                        mm.then_inc(x_used, 1)
                    if isinstance(b, int) and b == 0 and h == 0 and k == KX // 2:
                        pe.wait_ge(consts_ready, 1)
                        pe.wait_ge(att_reduced, NB)
                        nc.tensor.matmul(SET_B[0][:, 0:3 * NB], ones[:, :],
                                         att_sum[:, :, :].rearrange("p b j -> p (b j)"),
                                         start=True, stop=True).then_inc(att_done, 1)

            def z_group(b, h, grp, last=False):
                use = banks[(h + grp) % 2]
                for k in range(KY):
                    if grp == 0:
                        pe.wait_ge(y_lo_ready, KY * (2 * b + h) + k + 1)
                    for i in range(SET):
                        if k == 0:
                            if h == 0 and grp == 0:
                                if isinstance(b, int) and b == 0:
                                    pe.wait_ge(t_used_sem, i + 1)
                                else:
                                    pe.wait_ge(z_copied, 16 * (b - 1) + 12 + i + 1)
                            elif h == 0:
                                pe.wait_ge(t_used_sem, 4 * (2 * b + 1) + i + 1)
                            elif grp == 0:
                                pe.wait_ge(z_copied, 16 * b + 4 + i + 1)
                            elif last:
                                pe.wait_ge(z_copied, 16 * b + i + 1)
                            else:
                                pe.wait_ge(t_used_sem, 4 * (2 * b + 2) + i + 1)
                            if isinstance(b, int) and b == 0 and h == 0 and grp == 0 and i == 0:
                                pe.wait_ge(w_lo_ready, SLICES)
                        col = (4 * grp + i) * P
                        mm = three_pass(use[i][:, :], w_hi[:, KY + k, col:col + P], w_lo[:, KY + k, col:col + P],
                                        y_hi[:, h, k, :], y_lo[:, h, k, :], k == 0, k == KY - 1)
                        if k == KY - 1:
                            mm.then_inc(z_done, 1)

            t_used_sem = w_ready

            pg_image(0, 0)
            pg_image(1, 1)
            with pe.Fori(1, NB // 2) as c:
                pg_image(2 * c, 0)
                pg_image(2 * c + 1, 1)

            def body(b, last=False):
                t_group(b, 1)
                z_group(b, 0, 0)
                z_group(b, 0, 1)
                if not last:
                    t_group(b + 1, 0)
                z_group(b, 1, 0)
                z_group(b, 1, 1, last)

            t_group(0, 0)
            body(0)
            with pe.Fori(1, NB - 1) as b:
                body(b)
            body(NB - 1, last=True)

        @block.scalar
        def _(act):
            def a_split(raw, j):
                for k in range(KB):
                    nc.scalar.copy(split_t[:, 8 * j + k, :], raw[:, k, :]).then_inc(a_hi_ready, 1)

            def b_split(b, j, k):
                count = STAGES * b + j
                if isinstance(b, int) and b == 0 and j == 0:
                    act.wait_ge(b_first[k], 16)
                elif j == 0:
                    act.wait_ge(b_landed[R11], 16 * b)
                elif j in (2, 6):
                    act.wait_ge(b_landed[B_FROM[j]], 16 * b + 16)
                elif j == 1:
                    act.wait_ge(b_summed, 8 * b + 2 * (k // 2) + 2)
                elif j == 3:
                    act.wait_ge(b_summed, 8 * b + 5 + k // 2)
                elif j == 4:
                    act.wait_ge(b_summed, 8 * b + 2 * (k // 2) + 1)
                else:
                    act.wait_ge(b_summed, 8 * b + 7 + k // 2)
                if not (isinstance(b, int) and b == 0 and j == 0):
                    if k < KB - 1:
                        act.wait_ge(b_used, (KB - 1) * (count - 1) + k + 1)
                    else:
                        act.wait_ge(prod_done, SET * count)
                nc.scalar.copy(b_hi[:, k, :], flat_t[:, 4 * B_FROM[j] + k, :]).then_inc(b_hi_ready, 1)

            def copy_p1(b, i, odd):
                act.wait_ge(prod_done, SET * STAGES * b + i + 1)
                if isinstance(b, int) and b == 0:
                    act.wait_ge(a_summed, 8)
                    act.wait_ge(a_lo_ready, 3 * KB)
                else:
                    act.wait_ge(pair_summed, 8 * (b - 1) + PAIR_AT[C21] + 2)
                nc.scalar.copy(p1_buf[:, i, :], banks[odd][i][:, :]).then_inc(p1_copied, 1)

            def copy_g(b, n, odd):
                act.wait_ge(prod_done, SET * (STAGES * b + 2) + 2 * n + 2)
                if isinstance(b, int) and b == 0:
                    act.wait_ge(a_lo_ready, STAGES * KB)
                else:
                    act.wait_ge(pair_summed, 8 * (b - 1) + PAIR_AT[C11] + n + 1)
                    if n == 0:
                        act.wait_ge(att_reduced, b)
                nc.scalar.activation(tmp_a[:, n, :], banks[odd][2 * n + 1][:, :], ACT.Identity,
                                     accum_out=att_part[:, 0, n:n + 1]).then_inc(g_copied, 1)

            def pg_image(b, odd, last=False):
                for j in range(STAGES):
                    if isinstance(b, int) and b == 0:
                        if j == 0:
                            act.wait_ge(a_landed[1], 16)
                            a_split(a22_raw, 5)
                            act.wait_ge(a_summed, 6)
                            a_split(a11_raw, 1)
                        elif j == 1:
                            act.wait_ge(a_landed[3], 16)
                            a_split(a12_raw, 2)
                            act.wait_ge(a_summed, 8)
                            a_split(a12_raw, 6)
                        elif j == 2:
                            a_split(a21_raw, 3)
                            a_split(a22_raw, 4)
                    for k in range(KB):
                        if j == 1:
                            copy_p1(b, k, odd)
                        elif j == 3 and k < 2:
                            copy_g(b, k, odd)
                        if j < STAGES - 1:
                            b_split(b, j + 1, k)
                        elif not last:
                            b_split(b + 1, 0, k)
                    if last and j >= 4:
                        for s in ((), (), (), (), (0, 1), (2, 3), (4, 5))[j]:
                            split_w(s)

            def split_w(s):
                act.wait_ge(w_landed[s], 16)
                act.wait_ge(prod_done, SET * (STAGES * LAST + 4))
                nc.scalar.copy(w_hi[:, s, :], z_sb[:, s, :]).then_inc(w_hi_ready, 1)

            def split_x(b, h, q):
                act.wait_ge(x_landed[q], 16 * (2 * b + h) + 16)
                if isinstance(b, int) and b == 0 and h == 0:
                    act.wait_ge(prod_done, SET * (STAGES * LAST + 6))
                elif q < PAIRS - 1:
                    act.wait_ge(x_used, (PAIRS - 1) * (2 * b + h - 1) + q + 1)
                else:
                    act.wait_ge(t_done, KY * (2 * b + h))
                nc.scalar.copy(x_hi[:, 2 * q:2 * q + 2, :], x_raw[:, q, :, :]).then_inc(x_hi_ready, 1)

            def t_to_y(b, h):
                def u(i):
                    n = 4 * (2 * b + h) + i
                    act.wait_ge(t_done, n + 1)
                    if not (isinstance(b, int) and b == 0 and h == 0 and i < 2):
                        act.wait_ge(w_ready, n - 1)
                    else:
                        act.wait_ge(pair_summed, 8 * LAST + PAIR_AT[C11] + 2)
                        act.wait_ge(coef_ready, 1)
                    act.sem_inc(act_waited, 1)
                    nc.scalar.activation(tmp_a[:, i % 2, :], banks[h][i][:, :], ACT.Identity,
                                         bias=coef[:, b, 1:2], scale=coef[:, b, 2:3]).then_inc(u_ready, 1)

                def hi(i):
                    n = 4 * (2 * b + h) + i
                    act.wait_ge(w_ready, n + 1)
                    if not (isinstance(b, int) and b == 0):
                        act.wait_ge(z_done, 16 * (b - 1) + 8 * h + 8)
                    elif h == 0 and i == 0:
                        act.wait_ge(prod_done, SET * STAGES * NB)
                    nc.scalar.copy(y_hi[:, h, i, :], tmp_b[:, i % 2, :]).then_inc(y_hi_ready, 1)

                u(0)
                u(1)
                hi(0)
                u(2)
                hi(1)
                u(3)
                hi(2)
                hi(3)

            def copy_z(b, h, grp):
                for i in range(SET):
                    m = 4 * grp + i
                    act.wait_ge(z_done, 16 * b + 8 * h + m + 1)
                    if h == 0 and m == 0:
                        act.wait_ge(z_bias_ready, b + 1)
                    if h == 0 and not (isinstance(b, int) and b == 0):
                        act.wait_ge(fin_scaled, MZ * (b - 1) + m + 1)
                    nc.scalar.activation(z_sb[:, m, h * HALF:(h + 1) * HALF], banks[(h + grp) % 2][i][:, :],
                                         ACT.Identity, bias=z_bias[:, m:m + 1]).then_inc(z_copied, 1)

            def finish(b, m0, m1):
                for m in range(m0, m1):
                    act.wait_ge(fin_scaled, MZ * b + m + 1)
                    nc.scalar.activation(fin[:, m % NFIN, :], fin[:, m % NFIN, :], ACT.Identity,
                                         bias=shift_b[:, m:m + 1]).then_inc(fin_done, 1)
                    act.wait_ge(fin_done, MZ * b + m + 1)
                    act.dma_start(out_v[b, :, m, :], fin[:, m % NFIN, :]).then_inc(out_landed[m % NFIN], 16)

            for k in range(KB):
                act.wait_ge(a_landed[0], 16 * KB) if k == 0 else None
                nc.scalar.copy(split_t[:, k, :], a11_raw[:, k, :]).then_inc(a_hi_ready, 1)
                b_split(0, 0, k)
            pg_image(0, 0)
            pg_image(1, 1)
            with act.Fori(1, NB // 2 - 1) as c:
                pg_image(2 * c, 0)
                pg_image(2 * c + 1, 1)
            pg_image(LAST - 1, 0)
            pg_image(LAST, 1, last=True)

            def body(b, last=False):
                if not (isinstance(b, int) and b == 0):
                    copy_z(b - 1, 1, 1)
                    finish(b - 1, 0, NFIN)
                t_to_y(b, 1)
                if not last:
                    for q in range(PAIRS):
                        split_x(b + 1, 0, q)
                if not (isinstance(b, int) and b == 0):
                    finish(b - 1, NFIN, MZ)
                copy_z(b, 0, 0)
                copy_z(b, 0, 1)
                if not last:
                    t_to_y(b + 1, 0)
                    for q in range(PAIRS):
                        split_x(b + 1, 1, q)
                copy_z(b, 1, 0)

            for q in range(PAIRS):
                split_x(0, 0, q)
            for s in (6, 7):
                split_w(s)
            for q in range(PAIRS):
                split_x(0, 1, q)
            t_to_y(0, 0)
            body(0)
            with act.Fori(1, NB - 1) as b:
                body(b)
            body(NB - 1, last=True)
            copy_z(NB - 1, 1, 1)
            finish(NB - 1, 0, MZ)

        @block.vector
        def _(dve):
            def a_split(raw, j):
                for k in range(KB):
                    dve.wait_ge(a_hi_ready, KB * A_ORDER.index(j) + k + 1)
                    nc.vector.tensor_tensor(split_t[:, 8 * j + KB + k, :], raw[:, k, :],
                                            split_t[:, 8 * j + k, :].bitcast(FP32),
                                            ALU.subtract).then_inc(a_lo_ready, 1)

            def a_sum(dst, in0, in1, op):
                for c in range(0, KB, 2):
                    nc.vector.tensor_tensor(dst[:, c:c + 2, :], in0[:, c:c + 2, :], in1[:, c:c + 2, :],
                                            op).then_inc(a_summed, 1)

            def b_split(b, j, k):
                dve.wait_ge(b_hi_ready, KB * (STAGES * b + j) + k + 1)
                nc.vector.tensor_tensor(b_lo[:, k, :], flat_t[:, 4 * B_FROM[j] + k, :],
                                        b_hi[:, k, :].bitcast(FP32), ALU.subtract).then_inc(b_lo_ready, 1)

            def add_bank(b, what, src, dst, i, odd, acc=None):
                dve.wait_ge(prod_done, SET * (STAGES * b + what) + i + 1)
                nc.vector.scalar_tensor_tensor(out=dst[:, i, :], in0=banks[(what + odd) % 2][i][:, :], scalar=1.0,
                                               in1=src[:, i, :], op0=ALU.mult, op1=ALU.add,
                                               accum_out=acc).then_inc(bank_read, 1)

            def times(b, what, n, p_in, g_in, order):
                count = 8 * b + PAIR_AT[what] + n
                col = PAIR_AT[what] + n
                if order == 1 and not (isinstance(b, int) and count < 2):
                    dve.wait_ge(pair_summed, count - 1)
                if order == 2:
                    dve.wait_ge(pg_ready, count + 1)
                nc.vector.scalar_tensor_tensor(out=tmp_b[:, n, :], in0=p_in, scalar=1.0,
                                               in1=g_in, op0=ALU.mult, op1=ALU.mult,
                                               accum_out=att_part[:, order, col:col + 1]
                                               ).then_inc((pg_ready, pair_summed)[order - 1], 1)

            def evacuate(b, what, k, odd):
                if what == P6_SUM:
                    if k == 0:
                        dve.wait_ge(p1_copied, SET * b + SET)
                        if isinstance(b, int) and b == 0:
                            dve.wait_ge(a_lo_ready, 5 * KB)
                        else:
                            dve.wait_ge(pair_summed, 8 * b)
                    add_bank(b, what, p1_buf, sum6, k, odd)
                elif what == P67_SUM:
                    if k == 0:
                        if isinstance(b, int) and b == 0:
                            dve.wait_ge(a_lo_ready, 6 * KB)
                        else:
                            dve.wait_ge(pair_summed, 8 * (b - 1) + PAIR_AT[C22] + 2)
                    add_bank(b, what, p1_buf, sum67, k, odd)
                elif what == C11:
                    bank = banks[odd][2 * (k % 2)][:, :]
                    if k < 2:
                        dve.wait_ge(g_copied, 2 * b + k + 1)
                        times(b, what, k, bank, tmp_a[:, k, :], 1)
                    else:
                        times(b, what, k - 2, bank, tmp_b[:, k - 2, :], 2)
                elif what in (C22, C21, C12):
                    buf = {C22: sum67, C21: p1_buf, C12: sum6}[what]
                    base = READS * b + READ_AT[what]
                    if k < 2:
                        if k == 0 and what == C22:
                            dve.wait_ge(bank_read, READS * b + READ_AT[P67_SUM] + SET)
                        col = PAIR_AT[what] + k
                        add_bank(b, what, buf, buf, 2 * k, odd)
                        add_bank(b, what, buf, buf, 2 * k + 1, odd, att_part[:, 0, col:col + 1])
                    else:
                        if k == 2:
                            dve.wait_ge(bank_read, base + SET)
                        for n in range(2):
                            p_in = buf[:, 2 * n, :]
                            times(b, what, n, p_in, buf[:, 2 * n + 1, :] if k == 2 else tmp_b[:, n, :], k - 1)

            def reduce_sums(b):
                dve.wait_ge(pair_summed, 8 * b + 8)
                nc.vector.tensor_reduce(att_sum[:, b, :], att_part[:, :, :], AX.X, ALU.add).then_inc(att_reduced, 1)

            def pg_image(b, odd, last=False):
                for j in range(STAGES):
                    if isinstance(b, int) and b == 0:
                        if j == 0:
                            a_split(a22_raw, 5)
                            dve.wait_ge(a_landed[2], 16)
                            dve.wait_ge(a_lo_ready, 2 * KB)
                            dve.wait_ge(a_hi_ready, 2 * KB)
                            a_sum(a22_raw, a21_raw, a22_raw, ALU.add)
                            dve.wait_ge(a_summed, 2)
                            a_sum(a21_raw, a11_raw, a21_raw, ALU.subtract)
                            dve.wait_ge(a_summed, 4)
                            a_sum(a11_raw, a22_raw, a11_raw, ALU.subtract)
                            a_split(a11_raw, 1)
                        elif j == 1:
                            a_split(a12_raw, 2)
                            dve.wait_ge(a_lo_ready, 4 * KB)
                            a_sum(a12_raw, a12_raw, a11_raw, ALU.subtract)
                            a_split(a12_raw, 6)
                        elif j == 2:
                            a_split(a21_raw, 3)
                            a_split(a22_raw, 4)
                    for k in range(KB):
                        if j > 0:
                            evacuate(b, j - 1, k, odd)
                        elif not (isinstance(b, int) and b == 0):
                            evacuate(b - 1, C12, k, 1 - odd)
                        if j < STAGES - 1:
                            b_split(b, j + 1, k)
                        elif not last:
                            b_split(b + 1, 0, k)
                    if j == 0 and not (isinstance(b, int) and b == 0):
                        reduce_sums(b - 1)
                    if last and j >= 4:
                        for s in ((), (), (), (), (0, 1), (2, 3), (4, 5))[j]:
                            split_w(s)

            def split_w(s):
                dve.wait_ge(w_hi_ready, s + 1)
                nc.vector.tensor_tensor(w_lo[:, s, :], z_sb[:, s, :], w_hi[:, s, :].bitcast(FP32),
                                        ALU.subtract).then_inc(w_lo_ready, 1)

            def split_x(b, h, q):
                dve.wait_ge(x_hi_ready, PAIRS * (2 * b + h) + q + 1)
                nc.vector.tensor_tensor(x_lo[:, 2 * q:2 * q + 2, :], x_raw[:, q, :, :],
                                        x_hi[:, 2 * q:2 * q + 2, :].bitcast(FP32),
                                        ALU.subtract).then_inc(x_lo_ready, 1)

            def t_to_y(b, h):
                def w(i):
                    n = 4 * (2 * b + h) + i
                    dve.wait_ge(u_ready, n + 1)
                    if not (isinstance(b, int) and b == 0 and h == 0 and i < 2):
                        dve.wait_ge(y_lo_ready, n - 1)
                    nc.vector.tensor_tensor(tmp_b[:, i % 2, :], banks[h][i][:, :], tmp_a[:, i % 2, :],
                                            ALU.mult).then_inc(w_ready, 1)

                def lo(i):
                    n = 4 * (2 * b + h) + i
                    dve.wait_ge(y_hi_ready, n + 1)
                    nc.vector.tensor_tensor(y_lo[:, h, i, :], tmp_b[:, i % 2, :], y_hi[:, h, i, :].bitcast(FP32),
                                            ALU.subtract).then_inc(y_lo_ready, 1)

                w(0)
                w(1)
                lo(0)
                w(2)
                lo(1)
                w(3)
                lo(2)
                lo(3)

            def z_stats(b, h, grp):
                for i in range(SET):
                    m = 4 * grp + i
                    dve.wait_ge(z_copied, 16 * b + 8 * h + m + 1)
                    if h == 0 and m == 0 and not (isinstance(b, int) and b == 0):
                        dve.wait_ge(mv_ready, b)
                    nc.vector.bn_stats(stats[:, 8 * h + m, :],
                                       z_sb[:, m, h * HALF:(h + 1) * HALF]).then_inc(z_stat, 1)

            def image_stats(b):
                dve.wait_ge(z_stat, 16 * b + 16)
                if not (isinstance(b, int) and b == 0):
                    dve.wait_ge(ab_ready, b)
                dve.sem_inc(dve_waited, 1)
                nc.vector.bn_aggr(mean_var[:, :], stats[:, :, :].rearrange("p a b -> p (a b)")).then_inc(mv_ready, 1)

            def bias(b):
                if not (isinstance(b, int) and b == 0):
                    dve.wait_ge(z_copied, 16 * b)
                nc.vector.tensor_scalar(z_bias[:, :], wz_rowsum[:, :], coef[:, b, 0:1], None,
                                        ALU.mult).then_inc(z_bias_ready, 1)

            def scale(b, m0, m1):
                for m in range(m0, m1):
                    if m == m0:
                        dve.wait_ge(ab_ready, b + 1)
                    dve.wait_ge(res_landed[m % NFIN], 16 * (b * (MZ // NFIN) + m // NFIN) + 16)
                    nc.vector.scalar_tensor_tensor(out=fin[:, m % NFIN, :], in0=z_sb[:, m, :],
                                                   scalar=scale_a[:, m:m + 1], in1=fin[:, m % NFIN, :],
                                                   op0=ALU.mult, op1=ALU.add).then_inc(fin_scaled, 1)

            for k in range(KB):
                dve.wait_ge(a_hi_ready, k + 1)
                nc.vector.tensor_tensor(split_t[:, KB + k, :], a11_raw[:, k, :], split_t[:, k, :].bitcast(FP32),
                                        ALU.subtract).then_inc(a_lo_ready, 1)
                b_split(0, 0, k)
            pg_image(0, 0)
            pg_image(1, 1)
            with dve.Fori(1, NB // 2 - 1) as c:
                pg_image(2 * c, 0)
                pg_image(2 * c + 1, 1)
            pg_image(LAST - 1, 0)
            pg_image(LAST, 1, last=True)

            def body(b, last=False):
                if not (isinstance(b, int) and b == 0):
                    z_stats(b - 1, 1, 1)
                    image_stats(b - 1)
                if isinstance(b, int) and b == 0:
                    dve.wait_ge(wz_landed, 16)
                    nc.vector.tensor_reduce(wz_rowsum[:, :], fin.rearrange("p a (b c) -> p (a b) c", c=CP), AX.X,
                                            ALU.add).then_inc(rowsum_ready, 1)
                    dve.wait_ge(rowsum_ready, 1)
                bias(b)
                if not (isinstance(b, int) and b == 0):
                    scale(b - 1, 0, NFIN)
                t_to_y(b, 1)
                if not last:
                    for q in range(PAIRS):
                        split_x(b + 1, 0, q)
                if not (isinstance(b, int) and b == 0):
                    scale(b - 1, NFIN, MZ)
                z_stats(b, 0, 0)
                z_stats(b, 0, 1)
                if not last:
                    t_to_y(b + 1, 0)
                    for q in range(PAIRS):
                        split_x(b + 1, 1, q)
                z_stats(b, 1, 0)

            for q in range(PAIRS):
                split_x(0, 0, q)
            for k in range(KB):
                evacuate(LAST, C12, k, 1)
            reduce_sums(LAST)
            for s in (6, 7):
                split_w(s)
            for q in range(PAIRS):
                split_x(0, 1, q)
            dve.wait_ge(att_done, 1)
            nc.vector.tensor_tensor(coef[:, :, :].rearrange("p b j -> p (b j)"), SET_B[0][:, 0:3 * NB],
                                    alpha2[:, :, :].rearrange("p b j -> p (b j)"),
                                    ALU.mult).then_inc(coef_ready, 1)
            dve.wait_ge(coef_ready, 1)
            t_to_y(0, 0)
            body(0)
            with dve.Fori(1, NB - 1) as b:
                body(b)
            body(NB - 1, last=True)
            z_stats(NB - 1, 1, 1)
            image_stats(NB - 1)
            scale(NB - 1, 0, MZ)

        @block.gpsimd
        def _(pool):
            for j in range(3):
                nc.gpsimd.memset(alpha2[:, :, j:j + 1], ALPHA2[j])
            nc.gpsimd.memset(st[:, 7:8], -0.5)
            nc.gpsimd.memset(ones[:, :], 1.0).then_inc(consts_ready, 1)
            pool.wait_ge(consts_ready, 1)
            pool.wait_ge(gn_landed, 32)

            def channel_factors(b):
                def step(ins, n):
                    ins.then_inc(st_step, 1)
                    pool.wait_ge(st_step, G_STEPS * b + n)
                    pool.sem_inc(pool_waited, 1)

                pool.wait_ge(mv_ready, b + 1)
                pool.sem_inc(pool_waited, 1)
                step(nc.gpsimd.partition_all_reduce(st[:, 0:1], mean_var[:, 0:1], P, RADD), 1)
                step(nc.gpsimd.tensor_scalar(st[:, 1:2], st[:, 0:1], -1.0 / P, 0.0, ALU.mult, ALU.add), 2)
                step(nc.gpsimd.tensor_tensor(st[:, 2:3], mean_var[:, 0:1], st[:, 1:2], ALU.add), 3)
                step(nc.gpsimd.tensor_scalar(st[:, 3:4], st[:, 2:3], st[:, 2:3], mean_var[:, 1:2],
                                             ALU.mult, ALU.add), 4)
                step(nc.gpsimd.partition_all_reduce(st[:, 4:5], st[:, 3:4], P, RADD), 5)
                step(nc.gpsimd.tensor_scalar(st[:, 5:6], st[:, 4:5], 1.0 / P, EPS, ALU.mult, ALU.add), 6)
                step(nc.gpsimd.tensor_tensor(st[:, 6:7], st[:, 5:6], st[:, 7:8], ALU.pow), 7)
                if not (isinstance(b, int) and b == 0):
                    pool.wait_ge(fin_done, MZ * b)
                    pool.sem_inc(pool_waited, 1)
                nc.gpsimd.tensor_scalar(scale_a[:, :], gnw[:, :], st[:, 6:7], 1.0, ALU.mult, ALU.mult)
                step(nc.gpsimd.tensor_scalar(shift_t[:, :], gnw[:, :], st[:, 6:7], st[:, 1:2],
                                             ALU.mult, ALU.mult), 8)
                nc.gpsimd.tensor_tensor(shift_b[:, :], shift_t[:, :], gnb[:, :], ALU.add).then_inc(ab_ready, 1)

            def b_sum(dst, in0, in1, c, op):
                d, i0, i1 = (flat_t[:, 4 * buf + 2 * c:4 * buf + 2 * c + 2, :] for buf in (dst, in0, in1))
                nc.gpsimd.tensor_tensor(d, i0, i1, op).then_inc(b_summed, 1)

            def b_sums(b):
                for c in range(2):
                    pool.wait_ge(b_landed[R12], 16 * b + 16)
                    pool.wait_ge(b_lo_ready, KB * STAGES * b + 2 * c + 2)
                    b_sum(R11, R12, R11, c, ALU.subtract)
                    pool.wait_ge(b_landed[R22], 16 * b + 16)
                    pool.wait_ge(b_summed, 8 * b + 2 * c + 1)
                    b_sum(RT, R22, R11, c, ALU.subtract)
                for c in range(2):
                    pool.wait_ge(b_summed, 8 * b + 4)
                    b_sum(R12, R22, R12, c, ALU.subtract)
                for c in range(2):
                    pool.wait_ge(b_landed[R21], 16 * b + 16)
                    pool.wait_ge(b_lo_ready, KB * (STAGES * b + 1) + 2 * c + 2)
                    b_sum(RT, R21, RT, c, ALU.subtract)

            b_sums(0)
            with pool.Fori(1, NB) as b:
                b_sums(b)
            channel_factors(0)
            with pool.Fori(1, NB) as b:
                channel_factors(b)


_OUT_SHAPE = (NB, CIN, 32, 32)


def kernel(x, L0_conv_Wt, L0_conv_Wp, L0_conv_Wg, L0_conv_Wz, L0_conv_gn_w, L0_conv_gn_b):
    import numpy as _np
    import concourse.bacc as _bacc
    from concourse import mybir as _mybir
    from concourse.bass_utils import run_bass_kernel_spmd as _run

    nc = _bacc.Bacc("TRN2", target_bir_lowering=False, num_devices=1)
    given = {
        "x": x,
        "wt_t": _np.transpose(L0_conv_Wt),
        "wpg_t": _np.transpose(_np.stack([_np.reshape(w, (2, 2, P, CIN)) for w in (L0_conv_Wp, L0_conv_Wg)], 2),
                               (4, 0, 1, 2, 3)).reshape(CIN, 2, 4 * P),
        "wz": L0_conv_Wz,
        "wz_t": _np.transpose(L0_conv_Wz),
        "gn_w": _np.transpose(_np.reshape(L0_conv_gn_w, (MZ, P))),
        "gn_b": _np.transpose(_np.reshape(L0_conv_gn_b, (MZ, P))),
    }
    arrays = {f"in_{name}_dram": _np.ascontiguousarray(a) for name, a in given.items()}
    args = [nc.dram_tensor(name, a.shape, _mybir.dt.from_np(a.dtype), kind="ExternalInput").ap()
            for name, a in arrays.items()]
    out = nc.dram_tensor("out_0_dram", _OUT_SHAPE, FP32, kind="ExternalOutput").ap()
    rbf_nonlocal_block(nc, *args, out)
    r = _run(nc, [arrays], core_ids=[0])
    return r.results[0]["out_0_dram"]
```

```python
import math
from contextlib import ExitStack

import concourse.bass as bass
from concourse import mybir

P = 128
NB, CIN, CP, HW = 16, 1024, 512, 1024
EPS = 1e-5
GAMMA = 1e-4
HALF = 512
NH = HW // HALF
KX = CIN // P
KY = CP // P
MZ = CIN // P
PAIRS = KX // 2
SLICES = KX // 2
SET = 4
NFIN = 4

STAGES = 7
KB = KX // 2
R11, R12, R21, R22, RT = range(5)
B_FROM = (R11, RT, R21, R12, R11, RT, R22)
A_ORDER = (0, 5, 1, 2, 3, 6, 4)
AZ_ORDER = (0, 5, 1, 2, 6, 3, 4)
OPENS = (0, 1, 4)
KZ = KY // 2
Z_OPENS = (0, 1, 2, 4)
Z_READS = 24
ROWS = (4, 5, 6, 7, 0, 1, 2, 3)


def a_splits(j, k):
    if j in A_ORDER[1:3]:
        return KB + 2 * (k - k % 2) + 2 * (j == A_ORDER[2]) + k % 2 + 1
    return KB * A_ORDER.index(j) + k + 1


def z_order(b):
    return (0, 2, 1, 3, 4, 5, 6) if isinstance(b, int) and b == NB - 1 else tuple(range(STAGES))


def z_read_at(b, j):
    return Z_READS * b + SET * (j - 1)


P1_COPY, P6_SUM, C11, P67_SUM, C22, C21, C12 = range(7)
READS = 20
READ_AT = {P6_SUM: 0, P67_SUM: 4, C22: 8, C21: 12, C12: 16}
PAIR_AT = {C11: 0, C22: 2, C21: 4, C12: 6}
ALPHA2 = [(2 * GAMMA) ** o / math.factorial(o) * math.exp(-2 * GAMMA) for o in range(3)]

FP32 = mybir.dt.float32
FP32R = mybir.dt.float32r
ALU = mybir.AluOpType
ACT = mybir.ActivationFunctionType
AX = mybir.AxisListType
RADD = bass.bass_isa.ReduceOp.add


def rbf_nonlocal_block(nc, x, wt_t, wpg_t, wz, wz_t, gn_w, gn_b, out):
    x_v = x.rearrange("b (k p) h w -> b p k (h w)", p=P)
    out_v = out.rearrange("b (m p) h w -> b p m (h w)", p=P)
    wt_v = wt_t.rearrange("(k p) o -> p k o", p=P)
    wpg_v = wpg_t.rearrange("(k p) u o -> p k u o", p=P)
    wz_v = wz.rearrange("(m p) c -> p m c", p=P)
    wzt_v = wz_t.rearrange("(k p) o -> p k o", p=P)

    ctx = ExitStack()
    with ctx:
        def sb(name, shape, dt=FP32):
            return ctx.enter_context(nc.sbuf_tensor(name, shape, dt))

        def sem(name):
            return ctx.enter_context(nc.semaphore(name))

        with ExitStack() as phase1:
            split_a = phase1.enter_context(nc.sbuf_tensor("split_a", [P, 48, HALF], FP32R))
            with nc.sbuf_tensor("s2_raw", [P, KB, HALF], FP32) as s2_raw:
                pass
            split_b = phase1.enter_context(nc.sbuf_tensor("split_b", [P, 16, HALF], FP32R))
            flat_t = phase1.enter_context(nc.sbuf_tensor("flat_t", [P, 36, HALF], FP32))
        sum67, p1_buf, sum6 = flat_t[:, 20:24, :], flat_t[:, 24:28, :], flat_t[:, 28:32, :]
        a21_raw, a11_raw, a12_raw, a22_raw = (flat_t[:, i:i + 4, :] for i in (20, 24, 28, 32))
        tmp_a, tmp_b = flat_t[:, 32:34, :], flat_t[:, 34:36, :]
        a_parts = [split_a[:, 8 * j:8 * j + 8, :] for j in range(STAGES - 1)] + [split_b[:, 0:8, :]]
        a_hi, a_lo = [part[:, 0:KB, :] for part in a_parts], [part[:, KB:KX, :] for part in a_parts]
        b_hi, b_lo = split_b[:, 8:12, :], split_b[:, 12:16, :]
        w_hi = sb("w_hi", [P, SLICES, 2 * CP], FP32R)
        w_lo = sb("w_lo", [P, SLICES, 2 * CP], FP32R)
        x_hi = sb("x_hi", [P, 4, HALF], FP32R)
        x_lo = sb("x_lo", [P, 4, HALF], FP32R)
        wz_split = sb("wz_split", [P, 4 * STAGES, HALF], FP32R)
        fin_0 = sb("fin_0", [P, 2, HW])
        y_hi = sb("y_hi", [P, 4, HALF], FP32R)
        y_lo = sb("y_lo", [P, 4, HALF], FP32R)
        z_sb = sb("z_sb", [P, MZ, HW])
        x_raw = sb("x_raw", [P, 2, 2, HALF])
        y_raw = sb("y_raw", [P, 14, HALF])
        fin_1 = sb("fin_1", [P, 2, HW])
        fin = [buf[:, i, :] for buf in (fin_0, fin_1) for i in range(2)]
        last_fin = [x_raw[:, i, :, :].rearrange("p k n -> p (k n)") for i in range(2)]
        last_fin += [y_raw[:, 2 * i:2 * i + 2, :].rearrange("p k n -> p (k n)") for i in range(2)]
        Y11, Y21 = [y_raw[:, 0:2, :], y_raw[:, 4:6, :]], [y_raw[:, 2:4, :], y_raw[:, 6:8, :]]
        Y12, Y22, YT = (y_raw[:, i:i + 2, :] for i in (8, 10, 12))
        z11_raw, z12_raw, z21_raw, z22_raw = (
            z_sb[:, 4 + i, :].rearrange("p (k n) -> p k n", k=KZ) for i in range(4))
        att_part = sb("att_part", [P, 3, NH * KY])
        att_sum = sb("att_sum", [P, NB, 3])
        alpha2 = sb("alpha2", [P, NB, 3])
        coef = sb("coef", [P, NB, 3])
        ones = sb("ones", [P, P])
        wz_rowsum = sb("wz_rowsum", [P, MZ])
        z_bias = sb("z_bias", [P, MZ])
        stats = sb("stats", [P, MZ * NH, 6])
        mean_var = sb("mean_var", [P, 2])
        st = sb("st", [P, 8])
        gnw = sb("gnw", [P, MZ])
        gnb = sb("gnb", [P, MZ])
        scale_a = sb("scale_a", [P, MZ])
        shift_b = sb("shift_b", [P, MZ])
        shift_t = sb("shift_t", [P, MZ])

        banks = [[ctx.enter_context(nc.psum_tensor(f"bank_{s}{i}", [P, HALF], FP32))
                  for i in range(SET)] for s in "ab"]
        SET_A, SET_B = banks

        a22_landed, a21_landed, a12_landed = (sem(name) for name in ("a22_landed", "a21_landed", "a12_landed"))
        b_landed = [sem(f"b_landed{i}") for i in range(4)]
        a_first = [sem(f"a_first{k}") for k in range(KB)]
        b_first = [sem(f"b_first{k}") for k in range(KB)]
        a22_early, a21_early, b12_early, b22_early = (
            sem(name) for name in ("a22_early", "a21_early", "b12_early", "b22_early"))
        w_landed = [sem(f"w_landed{s}") for s in range(SLICES)]
        az_landed = [sem(f"az_landed{i}") for i in range(4)]
        x_landed = [sem(f"x_landed{i}") for i in range(2)]
        res_landed = [sem(f"res_landed{i}") for i in range(NFIN)]
        last_landed = [sem(f"last_landed{i}") for i in range(NFIN)]
        out_landed = [sem(f"out_landed{i}") for i in range(NFIN)]
        wz_landed = sem("wz_landed")
        gn_landed = sem("gn_landed")
        a_hi_ready = sem("a_hi_ready")
        a_lo_ready = sem("a_lo_ready")
        a_summed = sem("a_summed")
        s3_ready = sem("s3_ready")
        b_hi_ready = sem("b_hi_ready")
        b_lo_ready = sem("b_lo_ready")
        b_summed = sem("b_summed")
        b_used = sem("b_used")
        prod_done = sem("prod_done")
        p1_copied = sem("p1_copied")
        bank_read = sem("bank_read")
        g_copied = sem("g_copied")
        pg_ready = sem("pg_ready")
        pair_summed = sem("pair_summed")
        att_reduced = sem("att_reduced")
        att_done = sem("att_done")
        coef_ready = sem("coef_ready")
        rowsum_ready = sem("rowsum_ready")
        consts_ready = sem("consts_ready")
        w_hi_ready = sem("w_hi_ready")
        w_lo_ready = sem("w_lo_ready")
        az_hi_ready = sem("az_hi_ready")
        az_lo_ready = sem("az_lo_ready")
        az_summed = sem("az_summed")
        x_hi_ready = sem("x_hi_ready")
        x_lo_ready = sem("x_lo_ready")
        x_used = sem("x_used")
        t_done = sem("t_done")
        u_ready = sem("u_ready")
        w_ready = sem("w_ready")
        y_hi_ready = sem("y_hi_ready")
        y_lo_ready = sem("y_lo_ready")
        y_summed = sem("y_summed")
        z_done = sem("z_done")
        z1_copied = sem("z1_copied")
        z_read = sem("z_read")
        z_bias_ready = sem("z_bias_ready")
        z_stat = sem("z_stat")
        mv_ready = sem("mv_ready")
        st_step = sem("st_step")
        ab_ready = sem("ab_ready")
        fin_scaled = sem("fin_scaled")
        fin_done = sem("fin_done")

        act_waited = sem("act_waited")
        dve_waited = sem("dve_waited")
        pool_waited = sem("pool_waited")
        sp_waited = sem("sp_waited")

        block = ctx.enter_context(nc.Block())

        LAST = NB - 1
        G_STEPS = 8

        @block.sync
        def _(sp):
            def load_b(b):
                done = KB * STAGES * (b - 1)
                sp.wait_ge(b_summed, 8 * (b - 1) + 8)
                sp.wait_ge(b_lo_ready, done + KB * 3)
                sp.sem_inc(sp_waited, 1)
                sp.dma_start(flat_t[:, 4 * R21:4 * R21 + 4, :], x_v[b, :, KB:KX, 0:HALF]).then_inc(b_landed[R21], 16)
                sp.wait_ge(b_lo_ready, done + KB * 4)
                sp.sem_inc(sp_waited, 1)
                sp.dma_start(flat_t[:, 4 * R12:4 * R12 + 4, :], x_v[b, :, 0:KB, HALF:HW]).then_inc(b_landed[R12], 16)
                sp.wait_ge(b_lo_ready, done + KB * 5)
                sp.sem_inc(sp_waited, 1)
                sp.dma_start(flat_t[:, 4 * R11:4 * R11 + 4, :], x_v[b, :, 0:KB, 0:HALF]).then_inc(b_landed[R11], 16)
                sp.wait_ge(b_lo_ready, done + KB * 7)
                sp.sem_inc(sp_waited, 1)
                sp.dma_start(flat_t[:, 4 * R22:4 * R22 + 4, :], x_v[b, :, KB:KX, HALF:HW]).then_inc(b_landed[R22], 16)

            def load_x(b, h, q):
                count = PAIRS * (2 * b + h) + q
                if not (isinstance(count, int) and count < 2):
                    sp.wait_ge(x_lo_ready, count - 1)
                sp.dma_start(x_raw[:, q % 2, :, :],
                             x_v[b, :, 2 * q:2 * q + 2, h * HALF:(h + 1) * HALF]).then_inc(x_landed[q % 2], 16)

            def load_res(b, n):
                slot = n % NFIN
                if not (isinstance(b, int) and b == 0 and n < NFIN):
                    sp.wait_ge(out_landed[slot], 16 * (b * (MZ // NFIN) + n // NFIN))
                sp.dma_start(fin[slot], x_v[b, :, ROWS[n], :]).then_inc(res_landed[slot], 16)

            for k in range(KB):
                sp.dma_start(a11_raw[:, k, :], wpg_v[:, k, 0, :]).then_inc(a_first[k], 16)
                sp.dma_start(flat_t[:, 4 * R11 + k, :], x_v[0, :, k, 0:HALF]).then_inc(b_first[k], 16)
            for c, sems in ((0, (b12_early, a22_early, b22_early, a21_early)),
                            (2, (b_landed[R12], a22_landed, b_landed[R22], a21_landed))):
                sp.dma_start(flat_t[:, 4 * R12 + c:4 * R12 + c + 2, :],
                             x_v[0, :, c:c + 2, HALF:HW]).then_inc(sems[0], 16)
                sp.dma_start(a22_raw[:, c:c + 2, :], wpg_v[:, KB + c:KB + c + 2, 1, :]).then_inc(sems[1], 16)
                sp.dma_start(flat_t[:, 4 * R22 + c:4 * R22 + c + 2, :],
                             x_v[0, :, KB + c:KB + c + 2, HALF:HW]).then_inc(sems[2], 16)
                sp.dma_start(a21_raw[:, c:c + 2, :], wpg_v[:, c:c + 2, 1, :]).then_inc(sems[3], 16)
            sp.dma_start(a12_raw, wpg_v[:, KB:KX, 0, :]).then_inc(a12_landed, 16)
            sp.dma_start(flat_t[:, 4 * R21:4 * R21 + 4, :], x_v[0, :, KB:KX, 0:HALF]).then_inc(b_landed[R21], 16)
            sp.dma_start(gnw[:, :], gn_w).then_inc(gn_landed, 16)
            sp.dma_start(gnb[:, :], gn_b).then_inc(gn_landed, 16)
            with sp.Fori(1, NB) as b:
                load_b(b)

            done = KB * STAGES * LAST
            sp.wait_ge(b_lo_ready, done + KB * 5)
            for s in range(SLICES):
                sp.dma_start(z_sb[:, s, :].rearrange("p (k o) -> p k o", k=2),
                             wt_v[:, 2 * s:2 * s + 2, :]).then_inc(w_landed[s], 16)
            sp.wait_ge(b_lo_ready, done + KB * 6)
            load_x(0, 0, 0)
            load_x(0, 0, 1)
            sp.wait_ge(b_lo_ready, done + KB * 7)
            sp.dma_start(z11_raw, wzt_v[:, 0:KZ, 0:HALF]).then_inc(az_landed[0], 16)
            sp.dma_start(z22_raw, wzt_v[:, KZ:KY, HALF:CIN]).then_inc(az_landed[1], 16)
            sp.dma_start(z21_raw, wzt_v[:, 0:KZ, HALF:CIN]).then_inc(az_landed[2], 16)
            sp.dma_start(z12_raw, wzt_v[:, KZ:KY, 0:HALF]).then_inc(az_landed[3], 16)
            load_x(0, 0, 2)
            load_x(0, 0, 3)
            sp.wait_ge(att_reduced, NB)
            for i, buf in enumerate((fin_0, fin_1)):
                sp.dma_start(buf[:, :, :].rearrange("p a (b c) -> p (a b) c", c=CP),
                             wz_v[:, 4 * i:4 * i + 4, :]).then_inc(wz_landed, 16)
            for q in range(PAIRS):
                load_x(0, 1, q)

            def body(b):
                for q in range(PAIRS):
                    load_x(b + 1, 0, q)
                load_x(b + 1, 1, 0)
                if isinstance(b, int) and b == 0:
                    sp.wait_ge(rowsum_ready, 1)
                else:
                    for n in range(NFIN, MZ):
                        load_res(b - 1, n)
                for q in range(1, PAIRS):
                    load_x(b + 1, 1, q)
                for n in range(NFIN):
                    load_res(b, n)

            body(0)
            with sp.Fori(1, LAST) as b:
                body(b)
            for b in (LAST - 1, LAST):
                if b == LAST:
                    for n in range(NFIN):
                        load_res(b, n)
                for i, buf in enumerate(last_fin):
                    if b == LAST - 1 and i == 0:
                        sp.wait_ge(x_lo_ready, 2 * PAIRS * NB)
                    elif b == LAST - 1 and i == 2:
                        sp.wait_ge(y_lo_ready, KZ * STAGES * LAST)
                    elif b == LAST:
                        sp.wait_ge(out_landed[i], 16 * LAST * (MZ // NFIN))
                    sp.dma_start(buf, x_v[b, :, ROWS[NFIN + i], :]).then_inc(last_landed[i], 16)
            for n in range(MZ):
                sp.wait_ge(fin_done, MZ * LAST + n + 1)
                sp.dma_start(out_v[LAST, :, ROWS[n], :], (fin + last_fin)[n]).then_inc(out_landed[n % NFIN], 16)
            for slot in range(NFIN):
                sp.wait_ge(out_landed[slot], 16 * NB * (MZ // NFIN))

        @block.tensor
        def _(pe):
            def three_pass(bank, hi_w, lo_w, hi_x, lo_x, first, last, resumed=False):
                nc.tensor.matmul(bank, hi_w, hi_x, start=first, stop=False, skip_group_check=resumed)
                nc.tensor.matmul(bank, hi_w, lo_x, start=False, stop=False, skip_group_check=resumed)
                return nc.tensor.matmul(bank, lo_w, hi_x, start=False, stop=last, skip_group_check=resumed)

            def stage(b, j, odd):
                use = banks[(j + odd) % 2]
                count = STAGES * b + j
                for k in range(KB):
                    if isinstance(b, int) and b == 0:
                        pe.wait_ge(a_lo_ready, a_splits(j, k))
                    pe.wait_ge(b_lo_ready, KB * count + k + 1)
                    for i in range(SET):
                        if k == 0 and j == 0 and not (isinstance(b, int) and b == 0):
                            pe.wait_ge(bank_read, READS * (b - 1) + READ_AT[C21] + i + 1)
                        elif k == 0 and j == 1 and not (isinstance(b, int) and b == 0):
                            pe.wait_ge(bank_read, READS * (b - 1) + READ_AT[C12] + i + 1)
                        elif k == 0 and j == 2:
                            pe.wait_ge(p1_copied, SET * b + i + 1)
                        elif k == 0 and j == 3:
                            pe.wait_ge(bank_read, READS * b + READ_AT[P6_SUM] + i + 1)
                        elif k == 0 and j == 4 and i % 2 == 0:
                            pe.wait_ge(pair_summed, 8 * b + PAIR_AT[C11] + i // 2 + 1)
                        elif k == 0 and j == 5:
                            pe.wait_ge(bank_read, READS * b + READ_AT[P67_SUM] + i + 1)
                        elif k == 0 and j == 6:
                            pe.wait_ge(bank_read, READS * b + READ_AT[C22] + i + 1)
                        hi_a = a_hi[j][:, k, i * P:(i + 1) * P]
                        lo_a = a_lo[j][:, k, i * P:(i + 1) * P]
                        mm = three_pass(use[i][:, :], hi_a, lo_a, b_hi[:, k, :], b_lo[:, k, :],
                                        k == 0 and j in OPENS, k == KB - 1, j not in OPENS)
                        if k == KB - 1:
                            mm.then_inc(prod_done, 1)
                    if k < KB - 1:
                        mm.then_inc(b_used, 1)

            def pg_image(b, odd):
                for j in range(STAGES):
                    stage(b, j, odd)

            def t_group(b, h, use):
                half = 2 * b + h
                for k in range(KX):
                    if k % 2 == 0:
                        if isinstance(b, int) and b == 0 and h == 0:
                            pe.wait_ge(w_lo_ready, k // 2 + 1)
                        pe.wait_ge(x_lo_ready, PAIRS * half + k // 2 + 1)
                    for i in range(SET):
                        if k == 0 and isinstance(b, int) and b == 0:
                            pe.wait_ge(bank_read, READS * LAST + READ_AT[(C21, C12)[h]] + i + 1)
                            if h == 1 and i == 0:
                                pe.wait_ge(coef_ready, 1)
                        elif k == 0 and h == 0:
                            pe.wait_ge(w_ready, SET * (2 * b - 1) + i + 1)
                        elif k == 0:
                            pe.wait_ge(z_read, z_read_at(b - 1, 5) + i + 1)
                        col = (k % 2) * CP + i * P
                        mm = three_pass(use[i][:, :], w_hi[:, k // 2, col:col + P], w_lo[:, k // 2, col:col + P],
                                        x_hi[:, k % 4, :], x_lo[:, k % 4, :], k == 0, k == KX - 1)
                        if k == KX - 1:
                            mm.then_inc(t_done, 1)
                    if k % 2 == 1 and k < KX - 1:
                        mm.then_inc(x_used, 1)
                    if isinstance(b, int) and b == 0 and h == 0 and k == KX // 2:
                        pe.wait_ge(consts_ready, 1)
                        pe.wait_ge(att_reduced, NB)
                        nc.tensor.matmul(SET_B[0][:, 0:3 * NB], ones[:, :],
                                         att_sum[:, :, :].rearrange("p b j -> p (b j)"),
                                         start=True, stop=True).then_inc(att_done, 1)

            def z_stage(b, j, odd, last):
                use = banks[(odd + (j in (2, 4, 6))) % 2]
                at = z_order(b).index(j)
                for k in range(KZ):
                    if isinstance(b, int) and b == 0:
                        pe.wait_ge(az_lo_ready, KZ * AZ_ORDER.index(j) + k + 1)
                    pe.wait_ge(y_lo_ready, KZ * (STAGES * b + at) + k + 1)
                    for i in range(SET):
                        if k == 0 and j == 0:
                            if isinstance(b, int) and b == 0:
                                pe.wait_ge(w_ready, i + 1)
                            else:
                                pe.wait_ge(z_read, z_read_at(b - 1, 6) + i + 1)
                        elif k == 0 and j == 1:
                            pe.wait_ge(z1_copied, SET * b + i + 1)
                        elif k == 0 and j == 2:
                            pe.wait_ge(w_ready, SET * (2 * b + (1 if last else 2)) + i + 1)
                        elif k == 0:
                            pe.wait_ge(z_read, z_read_at(b, j - 2) + i + 1)
                        hi_a = wz_split[:, 4 * j + k, i * P:(i + 1) * P]
                        lo_a = wz_split[:, 4 * j + KZ + k, i * P:(i + 1) * P]
                        slot = 2 * ((at + odd) % 2) + k
                        mm = three_pass(use[i][:, :], hi_a, lo_a, y_hi[:, slot, :], y_lo[:, slot, :],
                                        k == 0 and j in Z_OPENS, k == KZ - 1, j not in Z_OPENS)
                        if k == KZ - 1:
                            mm.then_inc(z_done, 1)

            pg_image(0, 0)
            pg_image(1, 1)
            with pe.Fori(1, NB // 2) as c:
                pg_image(2 * c, 0)
                pg_image(2 * c + 1, 1)

            def body(b, odd, last=False):
                t_group(b, 1, banks[1 - odd])
                z_stage(b, 0, odd, last)
                if not last:
                    t_group(b + 1, 0, banks[1 - odd])
                for j in z_order(b)[1:]:
                    z_stage(b, j, odd, last)

            t_group(0, 0, SET_A)
            body(0, 0)
            body(1, 1)
            with pe.Fori(1, NB // 2 - 1) as c:
                body(2 * c, 0)
                body(2 * c + 1, 1)
            body(LAST - 1, 0)
            body(LAST, 1, last=True)

        @block.scalar
        def _(act):
            def a_split(raw, j, chunks=range(KB)):
                for k in chunks:
                    nc.scalar.copy(a_hi[j][:, k, :], raw[:, k, :]).then_inc(a_hi_ready, 1)

            def b_split(b, j, k):
                count = STAGES * b + j
                if isinstance(b, int) and b == 0 and j == 0:
                    act.wait_ge(b_first[k], 16)
                elif j == 0:
                    act.wait_ge(b_landed[R11], 16 * b)
                elif j in (2, 6):
                    act.wait_ge(b_landed[B_FROM[j]], 16 * b + 16)
                elif j == 1:
                    act.wait_ge(b_summed, 8 * b + 2 * (k // 2) + 2)
                elif j == 3:
                    act.wait_ge(b_summed, 8 * b + 5 + k // 2)
                elif j == 4:
                    act.wait_ge(b_summed, 8 * b + 2 * (k // 2) + 1)
                else:
                    act.wait_ge(b_summed, 8 * b + 7 + k // 2)
                if not (isinstance(b, int) and b == 0 and j == 0):
                    if k < KB - 1:
                        act.wait_ge(b_used, (KB - 1) * (count - 1) + k + 1)
                    else:
                        act.wait_ge(prod_done, SET * count)
                nc.scalar.copy(b_hi[:, k, :], flat_t[:, 4 * B_FROM[j] + k, :]).then_inc(b_hi_ready, 1)

            def copy_p1(b, i, odd):
                act.wait_ge(prod_done, SET * STAGES * b + i + 1)
                if isinstance(b, int) and b == 0:
                    act.wait_ge(a_summed, 4)
                    act.wait_ge(s3_ready, 2)
                else:
                    act.wait_ge(pair_summed, 8 * (b - 1) + PAIR_AT[C21] + 2)
                nc.scalar.copy(p1_buf[:, i, :], banks[odd][i][:, :]).then_inc(p1_copied, 1)

            def copy_g(b, n, odd):
                act.wait_ge(prod_done, SET * (STAGES * b + 2) + 2 * n + 2)
                if isinstance(b, int) and b == 0:
                    act.wait_ge(a_lo_ready, STAGES * KB)
                else:
                    act.wait_ge(pair_summed, 8 * (b - 1) + PAIR_AT[C11] + n + 1)
                    if n == 0:
                        act.wait_ge(att_reduced, b)
                nc.scalar.activation(tmp_a[:, n, :], banks[odd][2 * n + 1][:, :], ACT.Identity,
                                     accum_out=att_part[:, 0, n:n + 1]).then_inc(g_copied, 1)

            def pg_image(b, odd, last=False):
                for j in range(STAGES):
                    if isinstance(b, int) and b == 0:
                        if j == 0:
                            for c, landed in ((0, a22_early), (2, a22_landed)):
                                act.wait_ge(landed, 16)
                                a_split(a22_raw, 5, (c, c + 1))
                                act.wait_ge(a_summed, c + 2)
                                a_split(s2_raw, 1, (c, c + 1))
                                for k in (c, c + 1):
                                    b_split(b, 1, k)
                        elif j == 1:
                            act.wait_ge(a12_landed, 16)
                            a_split(a12_raw, 2)
                        elif j == 2:
                            act.wait_ge(s3_ready, 2)
                            a_split(a21_raw, 3)
                            act.wait_ge(a_summed, 6)
                            a_split(a12_raw, 6)
                        elif j == 3:
                            a_split(a22_raw, 4)
                    for k in range(KB):
                        if j == 1:
                            copy_p1(b, k, odd)
                        elif j == 3 and k < 2:
                            copy_g(b, k, odd)
                        if j < STAGES - 1 and not (isinstance(b, int) and b == 0 and j == 0):
                            b_split(b, j + 1, k)
                        elif j == STAGES - 1 and not last:
                            b_split(b + 1, 0, k)
                    if last and j == 5:
                        split_w(0)
                        split_w(1)

            def split_w(s):
                act.wait_ge(w_landed[s], 16)
                act.wait_ge(prod_done, SET * (STAGES * LAST + 2))
                nc.scalar.copy(w_hi[:, s, :], z_sb[:, s, :]).then_inc(w_hi_ready, 1)

            def split_x(b, h, q):
                n = PAIRS * (2 * b + h) + q
                act.wait_ge(x_landed[q % 2], 16 * (PAIRS // 2 * (2 * b + h) + q // 2) + 16)
                if isinstance(n, int) and n < 2:
                    act.wait_ge(prod_done, SET * (STAGES * LAST + 3))
                elif q >= 2:
                    act.wait_ge(x_used, (PAIRS - 1) * (2 * b + h) + q - 1)
                elif q == 0:
                    act.wait_ge(x_used, (PAIRS - 1) * (2 * b + h))
                else:
                    act.wait_ge(t_done, KY * (2 * b + h))
                at = 2 * (q % 2)
                nc.scalar.copy(x_hi[:, at:at + 2, :], x_raw[:, q % 2, :, :]).then_inc(x_hi_ready, 1)

            def t_to_u(b, h, odd):
                for i in range(SET):
                    n = SET * (2 * b + h) + i
                    act.wait_ge(t_done, n + 1)
                    if i == 0:
                        if h == 0 and not (isinstance(b, int) and b < 2):
                            act.wait_ge(z_done, SET * STAGES * (b - 1))
                        elif h == 1 and not (isinstance(b, int) and b == 0):
                            act.wait_ge(z_done, SET * STAGES * b)
                        else:
                            act.wait_ge(coef_ready, 1)
                    act.sem_inc(act_waited, 1)
                    block_of_w = (Y12, Y22)[i // 2] if h else (Y11, Y21)[i // 2][odd]
                    nc.scalar.activation(block_of_w[:, i % 2, :], banks[(odd, 1 - odd)[h]][i][:, :], ACT.Identity,
                                         bias=coef[:, b, 1:2], scale=coef[:, b, 2:3]).then_inc(u_ready, 1)

            def y_from(j, odd):
                return (Y11[odd], YT, Y21[odd], Y12, Y11[odd], YT, Y22)[j]

            def y_split(b, j, odd):
                at = z_order(b).index(j)
                for k in range(KZ):
                    if j in (0, 2):
                        act.wait_ge(w_ready, SET * 2 * b + j + k + 1)
                    elif j == 6:
                        act.wait_ge(w_ready, SET * (2 * b + 2))
                    else:
                        act.wait_ge(y_summed, 4 * b + {1: 2, 3: 3, 4: 1, 5: 4}[j])
                    if k == 0:
                        if isinstance(b, int) and STAGES * b + at < 2:
                            act.wait_ge(prod_done, SET * STAGES * NB)
                        else:
                            act.wait_ge(z_done, SET * (STAGES * b + at - 1))
                    slot = 2 * ((at + odd) % 2) + k
                    nc.scalar.copy(y_hi[:, slot, :], y_from(j, odd)[:, k, :]).then_inc(y_hi_ready, 1)

            def copy_z1(b, odd):
                for i in range(SET):
                    act.wait_ge(z_done, SET * STAGES * b + i + 1)
                    if isinstance(b, int) and b == 0:
                        act.wait_ge(az_lo_ready, KZ * STAGES)
                    else:
                        act.wait_ge(fin_scaled, MZ * (b - 1) + i + 1)
                    nc.scalar.copy(z_sb[:, SET + i, 0:HALF], banks[odd][i][:, :]).then_inc(z1_copied, 1)

            def finish(b, n0, n1):
                last = isinstance(b, int) and b == LAST
                late = isinstance(b, int) and b >= LAST - 1
                for n in range(n0, n1):
                    m = ROWS[n]
                    row = (fin + last_fin)[n if late else n % NFIN]
                    act.wait_ge(fin_scaled, MZ * b + n + 1)
                    nc.scalar.activation(row, row, ACT.Identity,
                                         bias=shift_b[:, m:m + 1]).then_inc(fin_done, 1)
                    if last:
                        continue
                    act.wait_ge(fin_done, MZ * b + n + 1)
                    act.dma_start(out_v[b, :, m, :], row).then_inc(out_landed[n % NFIN], 16)

            def az_split(raw, j):
                if j == 0:
                    act.wait_ge(prod_done, SET * STAGES * NB)
                for k in range(KZ):
                    nc.scalar.copy(wz_split[:, 4 * j + k, :], raw[:, k, :]).then_inc(az_hi_ready, 1)

            for k in range(KB):
                act.wait_ge(a_first[k], 16)
                nc.scalar.copy(a_hi[0][:, k, :], a11_raw[:, k, :]).then_inc(a_hi_ready, 1)
                b_split(0, 0, k)
            pg_image(0, 0)
            pg_image(1, 1)
            with act.Fori(1, NB // 2 - 1) as c:
                pg_image(2 * c, 0)
                pg_image(2 * c + 1, 1)
            pg_image(LAST - 1, 0)
            pg_image(LAST, 1, last=True)

            split_x(0, 0, 0)
            split_x(0, 0, 1)
            split_w(2)
            split_w(3)
            split_x(0, 0, 2)
            act.wait_ge(az_landed[0], 16)
            az_split(z11_raw, 0)
            act.wait_ge(az_landed[1], 16)
            az_split(z22_raw, 5)
            split_x(0, 0, 3)
            act.wait_ge(az_summed, 3)
            az_split(z11_raw, 1)
            split_x(0, 1, 0)
            split_x(0, 1, 1)
            t_to_u(0, 0, 0)
            y_split(0, 0, 0)

            def body(b, odd, last=False):
                first = isinstance(b, int) and b == 0
                split_x(b, 1, 2)
                if first:
                    act.wait_ge(az_landed[3], 16)
                    az_split(z12_raw, 2)
                    act.wait_ge(az_summed, 4)
                    az_split(z12_raw, 6)
                split_x(b, 1, 3)
                if first:
                    az_split(z21_raw, 3)
                    az_split(z22_raw, 4)
                if not last:
                    split_x(b + 1, 0, 0)
                    split_x(b + 1, 0, 1)
                t_to_u(b, 1, odd)
                if last:
                    y_split(b, 2, odd)
                    copy_z1(b, odd)
                    y_split(b, 1, odd)
                    finish(b - 1, 0, 1)
                    y_split(b, 3, odd)
                    finish(b - 1, 1, 2)
                elif not first:
                    finish(b - 1, 0, 2)
                if not last:
                    split_x(b + 1, 0, 2)
                if not first:
                    finish(b - 1, 2, 4)
                if not last:
                    split_x(b + 1, 0, 3)
                    y_split(b, 1, odd)
                    copy_z1(b, odd)
                    y_split(b, 2, odd)
                if not last:
                    t_to_u(b + 1, 0, 1 - odd)
                for j in range(3, STAGES):
                    if not (last and j == 3):
                        y_split(b, j, odd)
                    if not first:
                        finish(b - 1, j + 1, j + 2)
                    if not last and j in (4, 5):
                        split_x(b + 1, 1, j - 4)
                if not last:
                    y_split(b + 1, 0, 1 - odd)

            body(0, 0)
            body(1, 1)
            with act.Fori(1, NB // 2 - 1) as c:
                body(2 * c, 0)
                body(2 * c + 1, 1)
            body(LAST - 1, 0)
            body(LAST, 1, last=True)
            finish(LAST, 0, MZ)

        @block.vector
        def _(dve):
            def a_split(raw, j, chunks=range(KB)):
                for k in chunks:
                    dve.wait_ge(a_hi_ready, a_splits(j, k))
                    nc.vector.tensor_tensor(a_lo[j][:, k, :], raw[:, k, :],
                                            a_hi[j][:, k, :].bitcast(FP32),
                                            ALU.subtract).then_inc(a_lo_ready, 1)

            def a_sum(dst, in0, in1, c, op):
                nc.vector.tensor_tensor(dst[:, c:c + 2, :], in0[:, c:c + 2, :], in1[:, c:c + 2, :],
                                        op).then_inc(a_summed, 1)

            def b_split(b, j, k):
                dve.wait_ge(b_hi_ready, KB * (STAGES * b + j) + k + 1)
                nc.vector.tensor_tensor(b_lo[:, k, :], flat_t[:, 4 * B_FROM[j] + k, :],
                                        b_hi[:, k, :].bitcast(FP32), ALU.subtract).then_inc(b_lo_ready, 1)

            def add_bank(b, what, src, dst, i, odd, acc=None):
                dve.wait_ge(prod_done, SET * (STAGES * b + what) + i + 1)
                nc.vector.scalar_tensor_tensor(out=dst[:, i, :], in0=banks[(what + odd) % 2][i][:, :], scalar=1.0,
                                               in1=src[:, i, :], op0=ALU.mult, op1=ALU.add,
                                               accum_out=acc).then_inc(bank_read, 1)

            def times(b, what, n, p_in, g_in, order):
                count = 8 * b + PAIR_AT[what] + n
                col = PAIR_AT[what] + n
                if order == 1 and not (isinstance(b, int) and count < 2):
                    dve.wait_ge(pair_summed, count - 1)
                if order == 2:
                    dve.wait_ge(pg_ready, count + 1)
                nc.vector.scalar_tensor_tensor(out=tmp_b[:, n, :], in0=p_in, scalar=1.0,
                                               in1=g_in, op0=ALU.mult, op1=ALU.mult,
                                               accum_out=att_part[:, order, col:col + 1]
                                               ).then_inc((pg_ready, pair_summed)[order - 1], 1)

            def evacuate(b, what, k, odd):
                if what == P6_SUM:
                    if k == 0:
                        dve.wait_ge(p1_copied, SET * b + SET)
                        if isinstance(b, int) and b == 0:
                            dve.wait_ge(a_lo_ready, 6 * KB)
                        else:
                            dve.wait_ge(pair_summed, 8 * b)
                    add_bank(b, what, p1_buf, sum6, k, odd)
                elif what == P67_SUM:
                    if k == 0:
                        if isinstance(b, int) and b == 0:
                            dve.wait_ge(a_lo_ready, 5 * KB)
                        else:
                            dve.wait_ge(pair_summed, 8 * (b - 1) + PAIR_AT[C22] + 2)
                    add_bank(b, what, p1_buf, sum67, k, odd)
                elif what == C11:
                    bank = banks[odd][2 * (k % 2)][:, :]
                    if k < 2:
                        dve.wait_ge(g_copied, 2 * b + k + 1)
                        times(b, what, k, bank, tmp_a[:, k, :], 1)
                    else:
                        times(b, what, k - 2, bank, tmp_b[:, k - 2, :], 2)
                elif what in (C22, C21, C12):
                    buf = {C22: sum67, C21: p1_buf, C12: sum6}[what]
                    base = READS * b + READ_AT[what]
                    if k < 2:
                        if k == 0 and what == C22:
                            dve.wait_ge(bank_read, READS * b + READ_AT[P67_SUM] + SET)
                        col = PAIR_AT[what] + k
                        add_bank(b, what, buf, buf, 2 * k, odd)
                        add_bank(b, what, buf, buf, 2 * k + 1, odd, att_part[:, 0, col:col + 1])
                    else:
                        if k == 2:
                            dve.wait_ge(bank_read, base + SET)
                        for n in range(2):
                            p_in = buf[:, 2 * n, :]
                            times(b, what, n, p_in, buf[:, 2 * n + 1, :] if k == 2 else tmp_b[:, n, :], k - 1)

            def reduce_sums(b):
                dve.wait_ge(pair_summed, 8 * b + 8)
                nc.vector.tensor_reduce(att_sum[:, b, :], att_part[:, :, :], AX.X, ALU.add).then_inc(att_reduced, 1)

            def pg_image(b, odd, last=False):
                for j in range(STAGES):
                    if isinstance(b, int) and b == 0:
                        if j == 0:
                            for c, landed in ((0, a21_early), (2, a21_landed)):
                                a_split(a22_raw, 5, (c, c + 1))
                                dve.wait_ge(landed, 16)
                                dve.wait_ge(a_lo_ready, KB + 2 * c + 2)
                                a_sum(a22_raw, a21_raw, a22_raw, c, ALU.add)
                                dve.wait_ge(a_summed, c + 1)
                                a_sum(s2_raw, a22_raw, a11_raw, c, ALU.subtract)
                                a_split(s2_raw, 1, (c, c + 1))
                                for k in (c, c + 1):
                                    b_split(b, 1, k)
                        elif j == 1:
                            for c in (0, 2):
                                a_split(a12_raw, 2, (c, c + 1))
                        elif j == 2:
                            a_split(a21_raw, 3)
                            a_split(a12_raw, 6)
                        elif j == 3:
                            a_split(a22_raw, 4)
                    for k in range(KB):
                        if j > 0:
                            evacuate(b, j - 1, k, odd)
                        elif not (isinstance(b, int) and b == 0):
                            evacuate(b - 1, C12, k, 1 - odd)
                        if j < STAGES - 1 and not (isinstance(b, int) and b == 0 and j == 0):
                            b_split(b, j + 1, k)
                        elif j == STAGES - 1 and not last:
                            b_split(b + 1, 0, k)
                        if isinstance(b, int) and b == 0 and j == 1 and k % 2 == 1:
                            dve.wait_ge(a_lo_ready, 4 * KB)
                            a_sum(a12_raw, a12_raw, s2_raw, k - 1, ALU.subtract)
                    if j == 0 and not (isinstance(b, int) and b == 0):
                        reduce_sums(b - 1)
                    if last and j == 5:
                        split_w(0)
                        split_w(1)
                        split_x(0, 0, 0)

            def split_w(s):
                dve.wait_ge(w_hi_ready, s + 1)
                nc.vector.tensor_tensor(w_lo[:, s, :], z_sb[:, s, :], w_hi[:, s, :].bitcast(FP32),
                                        ALU.subtract).then_inc(w_lo_ready, 1)

            def split_x(b, h, q):
                dve.wait_ge(x_hi_ready, PAIRS * (2 * b + h) + q + 1)
                at = 2 * (q % 2)
                nc.vector.tensor_tensor(x_lo[:, at:at + 2, :], x_raw[:, q % 2, :, :],
                                        x_hi[:, at:at + 2, :].bitcast(FP32), ALU.subtract).then_inc(x_lo_ready, 1)

            def u_to_w(b, h, odd):
                for i in range(SET):
                    dve.wait_ge(u_ready, SET * (2 * b + h) + i + 1)
                    w = ((Y12, Y22)[i // 2] if h else (Y11, Y21)[i // 2][odd])[:, i % 2, :]
                    nc.vector.tensor_tensor(w, banks[(odd, 1 - odd)[h]][i][:, :], w, ALU.mult).then_inc(w_ready, 1)

            def y_split(b, j, k, odd):
                at = z_order(b).index(j)
                dve.wait_ge(y_hi_ready, KZ * (STAGES * b + at) + k + 1)
                slot = 2 * ((at + odd) % 2) + k
                raw = (Y11[odd], YT, Y21[odd], Y12, Y11[odd], YT, Y22)[j]
                nc.vector.tensor_tensor(y_lo[:, slot, :], raw[:, k, :], y_hi[:, slot, :].bitcast(FP32),
                                        ALU.subtract).then_inc(y_lo_ready, 1)

            def read_z(b, j, i, odd):
                at = z_order(b).index(j)
                dve.wait_ge(z_done, SET * (STAGES * b + at) + i + 1)
                bank = banks[(odd + (j in (2, 4, 6))) % 2][i][:, :]
                p1 = z_sb[:, SET + i, 0:HALF]
                dst = {1: z_sb[:, i, HALF:HW], 2: z_sb[:, i, 0:HALF], 3: z_sb[:, SET + i, HALF:HW],
                       4: z_sb[:, SET + i, HALF:HW], 5: p1, 6: z_sb[:, i, HALF:HW]}[j]
                src = p1 if j in (1, 2, 3, 5) else dst
                if j == 1 and not (isinstance(b, int) and b == 0):
                    dve.wait_ge(fin_scaled, MZ * (b - 1) + SET + i + 1)
                if j == 2 and i == 0:
                    dve.wait_ge(z_bias_ready, b + 1)
                elif j == 4:
                    dve.wait_ge(z_read, z_read_at(b, 3) + i + 1)
                elif j == 6:
                    dve.wait_ge(z_read, z_read_at(b, 1) + i + 1)
                if j in (1, 2, 3):
                    dve.wait_ge(z1_copied, SET * b + i + 1)
                m = i if j in (2, 6) else SET + i
                bias = 0.0 if j in (1, 3) else z_bias[:, m:m + 1]
                nc.vector.scalar_tensor_tensor(out=dst, in0=bank, scalar=bias, in1=src, op0=ALU.add,
                                               op1=ALU.add).then_inc(z_read, 1)

            def z_stats(b, j, tiles=range(SET)):
                half = 0 if j in (2, 5) else 1
                for i in tiles:
                    m = i if j in (2, 6) else SET + i
                    dve.wait_ge(z_read, z_read_at(b, j) + i + 1)
                    if j == 2 and i == 0 and not (isinstance(b, int) and b == 0):
                        dve.wait_ge(mv_ready, b)
                    nc.vector.bn_stats(stats[:, 8 * half + m, :],
                                       z_sb[:, m, half * HALF:(half + 1) * HALF]).then_inc(z_stat, 1)

            def image_stats(b):
                dve.wait_ge(z_stat, 16 * b + 16)
                if not (isinstance(b, int) and b == 0):
                    dve.wait_ge(ab_ready, b)
                dve.sem_inc(dve_waited, 1)
                nc.vector.bn_aggr(mean_var[:, :], stats[:, :, :].rearrange("p a b -> p (a b)")).then_inc(mv_ready, 1)

            def bias(b):
                if not (isinstance(b, int) and b == 0):
                    dve.wait_ge(z_read, Z_READS * b)
                nc.vector.tensor_scalar(z_bias[:, :], wz_rowsum[:, :], coef[:, b, 0:1], None,
                                        ALU.mult).then_inc(z_bias_ready, 1)

            def scale(b, n0, n1):
                late = isinstance(b, int) and b >= LAST - 1
                for n in range(n0, n1):
                    m = ROWS[n]
                    row = (fin + last_fin)[n if late else n % NFIN]
                    if n == n0:
                        dve.wait_ge(ab_ready, b + 1)
                    if late and n >= NFIN:
                        dve.wait_ge(last_landed[n - NFIN], 16 * (b - LAST + 2))
                    elif isinstance(b, int) and b == LAST:
                        dve.wait_ge(res_landed[n], 16 * b * (MZ // NFIN))
                    else:
                        dve.wait_ge(res_landed[n % NFIN], 16 * (b * (MZ // NFIN) + n // NFIN) + 16)
                    nc.vector.scalar_tensor_tensor(out=row, in0=z_sb[:, m, :],
                                                   scalar=scale_a[:, m:m + 1], in1=row,
                                                   op0=ALU.mult, op1=ALU.add).then_inc(fin_scaled, 1)

            def az_split(raw, j):
                for k in range(KZ):
                    dve.wait_ge(az_hi_ready, KZ * AZ_ORDER.index(j) + k + 1)
                    nc.vector.tensor_tensor(wz_split[:, 4 * j + KZ + k, :], raw[:, k, :],
                                            wz_split[:, 4 * j + k, :].bitcast(FP32),
                                            ALU.subtract).then_inc(az_lo_ready, 1)

            def az_sum(dst, in0, in1, op):
                nc.vector.tensor_tensor(dst, in0, in1, op).then_inc(az_summed, 1)

            for k in range(KB):
                dve.wait_ge(a_hi_ready, a_splits(0, k))
                nc.vector.tensor_tensor(a_lo[0][:, k, :], a11_raw[:, k, :], a_hi[0][:, k, :].bitcast(FP32),
                                        ALU.subtract).then_inc(a_lo_ready, 1)
                b_split(0, 0, k)
            pg_image(0, 0)
            pg_image(1, 1)
            with dve.Fori(1, NB // 2 - 1) as c:
                pg_image(2 * c, 0)
                pg_image(2 * c + 1, 1)
            pg_image(LAST - 1, 0)
            pg_image(LAST, 1, last=True)

            split_x(0, 0, 1)
            split_w(2)
            split_w(3)
            for k in range(KB):
                evacuate(LAST, C12, k, 1)
            reduce_sums(LAST)
            split_x(0, 0, 2)
            az_split(z11_raw, 0)
            az_split(z22_raw, 5)
            split_x(0, 0, 3)
            dve.wait_ge(az_landed[2], 16)
            dve.wait_ge(az_lo_ready, 2 * KZ)
            az_sum(z22_raw, z21_raw, z22_raw, ALU.add)
            dve.wait_ge(az_summed, 1)
            az_sum(z21_raw, z11_raw, z21_raw, ALU.subtract)
            dve.wait_ge(az_summed, 2)
            az_sum(z11_raw, z22_raw, z11_raw, ALU.subtract)
            az_split(z11_raw, 1)
            dve.wait_ge(att_done, 1)
            nc.vector.tensor_tensor(coef[:, :, :].rearrange("p b j -> p (b j)"), SET_B[0][:, 0:3 * NB],
                                    alpha2[:, :, :].rearrange("p b j -> p (b j)"),
                                    ALU.mult).then_inc(coef_ready, 1)
            dve.wait_ge(coef_ready, 1)
            split_x(0, 1, 0)
            split_x(0, 1, 1)
            u_to_w(0, 0, 0)
            for k in range(KZ):
                y_split(0, 0, k, 0)

            def body(b, odd, last=False):
                first = isinstance(b, int) and b == 0
                if not first:
                    for i in range(SET):
                        read_z(b - 1, 6, i, 1 - odd)
                    z_stats(b - 1, 2)
                split_x(b, 1, 2)
                if first:
                    az_split(z12_raw, 2)
                    dve.wait_ge(az_lo_ready, 4 * KZ)
                    az_sum(z12_raw, z12_raw, z11_raw, ALU.subtract)
                    az_split(z12_raw, 6)
                else:
                    z_stats(b - 1, 4)
                    z_stats(b - 1, 5)
                split_x(b, 1, 3)
                if first:
                    az_split(z21_raw, 3)
                    az_split(z22_raw, 4)
                    dve.wait_ge(wz_landed, 32)
                    for i, buf in enumerate((fin_0, fin_1)):
                        ins = nc.vector.tensor_reduce(wz_rowsum[:, 4 * i:4 * i + 4],
                                                      buf[:, :, :].rearrange("p a (b c) -> p (a b) c", c=CP),
                                                      AX.X, ALU.add)
                    ins.then_inc(rowsum_ready, 1)
                    dve.wait_ge(rowsum_ready, 1)
                else:
                    z_stats(b - 1, 6)
                    image_stats(b - 1)
                bias(b)
                if not last:
                    split_x(b + 1, 0, 0)
                    split_x(b + 1, 0, 1)
                u_to_w(b, 1, odd)
                if last:
                    for k in range(KZ):
                        y_split(b, 2, k, odd)
                if not first:
                    scale(b - 1, 0, 4)
                if not last:
                    split_x(b + 1, 0, 2)
                    split_x(b + 1, 0, 3)
                    for k in range(KZ):
                        y_split(b, 1, k, odd)
                    for k in range(KZ):
                        y_split(b, 2, k, odd)
                else:
                    scale(b - 1, 4, 5)
                    for k in range(KZ):
                        y_split(b, 1, k, odd)
                if not first:
                    scale(b - 1, 5 if last else 4, MZ)
                if last:
                    for k in range(KZ):
                        y_split(b, 3, k, odd)
                if not last:
                    u_to_w(b + 1, 0, 1 - odd)
                for j in range(2, STAGES):
                    read_z(b, j - 1, 0, odd)
                    for k in range(KZ):
                        if j < STAGES - 1:
                            if not last:
                                y_split(b, j + 1, k, odd)
                        elif not last:
                            y_split(b + 1, 0, k, 1 - odd)
                        read_z(b, j - 1, k + 1, odd)
                    read_z(b, j - 1, 3, odd)
                    if not last and j in (4, 5):
                        split_x(b + 1, 1, j - 4)
                    if last and j > 3:
                        z_stats(b, (2, 4, 5)[j - 4])

            body(0, 0)
            body(1, 1)
            with dve.Fori(1, NB // 2 - 1) as c:
                body(2 * c, 0)
                body(2 * c + 1, 1)
            body(LAST - 1, 0)
            body(LAST, 1, last=True)
            for i in range(SET):
                read_z(LAST, 6, i, 1)
                z_stats(LAST, 6, (i,))
            image_stats(LAST)
            scale(LAST, 0, MZ)

        @block.gpsimd
        def _(pool):
            for j in range(3):
                nc.gpsimd.memset(alpha2[:, :, j:j + 1], ALPHA2[j])
            nc.gpsimd.memset(st[:, 7:8], -0.5)
            nc.gpsimd.memset(ones[:, :], 1.0).then_inc(consts_ready, 1)

            def channel_factors(b):
                def step(ins, n):
                    ins.then_inc(st_step, 1)
                    pool.wait_ge(st_step, G_STEPS * b + n)
                    pool.sem_inc(pool_waited, 1)

                pool.wait_ge(mv_ready, b + 1)
                pool.sem_inc(pool_waited, 1)
                step(nc.gpsimd.partition_all_reduce(st[:, 0:1], mean_var[:, 0:1], P, RADD), 1)
                step(nc.gpsimd.tensor_scalar(st[:, 1:2], st[:, 0:1], -1.0 / P, 0.0, ALU.mult, ALU.add), 2)
                step(nc.gpsimd.tensor_tensor(st[:, 2:3], mean_var[:, 0:1], st[:, 1:2], ALU.add), 3)
                step(nc.gpsimd.tensor_scalar(st[:, 3:4], st[:, 2:3], st[:, 2:3], mean_var[:, 1:2],
                                             ALU.mult, ALU.add), 4)
                step(nc.gpsimd.partition_all_reduce(st[:, 4:5], st[:, 3:4], P, RADD), 5)
                step(nc.gpsimd.tensor_scalar(st[:, 5:6], st[:, 4:5], 1.0 / P, EPS, ALU.mult, ALU.add), 6)
                step(nc.gpsimd.tensor_tensor(st[:, 6:7], st[:, 5:6], st[:, 7:8], ALU.pow), 7)
                if not (isinstance(b, int) and b == 0):
                    pool.wait_ge(fin_done, MZ * b)
                    pool.sem_inc(pool_waited, 1)
                nc.gpsimd.tensor_scalar(scale_a[:, :], gnw[:, :], st[:, 6:7], 1.0, ALU.mult, ALU.mult)
                step(nc.gpsimd.tensor_scalar(shift_t[:, :], gnw[:, :], st[:, 6:7], st[:, 1:2],
                                             ALU.mult, ALU.mult), 8)
                nc.gpsimd.tensor_tensor(shift_b[:, :], shift_t[:, :], gnb[:, :], ALU.add).then_inc(ab_ready, 1)

            def b_sum(dst, in0, in1, c, op):
                d, i0, i1 = (flat_t[:, 4 * buf + 2 * c:4 * buf + 2 * c + 2, :] for buf in (dst, in0, in1))
                nc.gpsimd.tensor_tensor(d, i0, i1, op).then_inc(b_summed, 1)

            def b_sums(b):
                for c in range(2):
                    if isinstance(b, int) and c == 0:
                        pool.wait_ge(b12_early, 16)
                    else:
                        pool.wait_ge(b_landed[R12], 16 * b + 16)
                    pool.wait_ge(b_lo_ready, KB * STAGES * b + 2 * c + 2)
                    b_sum(R11, R12, R11, c, ALU.subtract)
                    if isinstance(b, int) and c == 0:
                        pool.wait_ge(b22_early, 16)
                    else:
                        pool.wait_ge(b_landed[R22], 16 * b + 16)
                    pool.wait_ge(b_summed, 8 * b + 2 * c + 1)
                    b_sum(RT, R22, R11, c, ALU.subtract)
                if isinstance(b, int):
                    for c in (0, 2):
                        pool.wait_ge(a_summed, c + 1)
                        nc.gpsimd.tensor_tensor(a21_raw[:, c:c + 2, :], a11_raw[:, c:c + 2, :],
                                                a21_raw[:, c:c + 2, :], ALU.subtract).then_inc(s3_ready, 1)
                for c in range(2):
                    pool.wait_ge(b_summed, 8 * b + 4)
                    b_sum(R12, R22, R12, c, ALU.subtract)
                for c in range(2):
                    pool.wait_ge(b_landed[R21], 16 * b + 16)
                    pool.wait_ge(b_lo_ready, KB * (STAGES * b + 1) + 2 * c + 2)
                    b_sum(RT, R21, RT, c, ALU.subtract)

            b_sums(0)
            with pool.Fori(1, NB) as b:
                b_sums(b)

            def y_sum(dst, in0, in1):
                nc.gpsimd.tensor_tensor(dst, in0, in1, ALU.subtract).then_inc(y_summed, 1)

            def y_sums(b, odd):
                pool.wait_ge(w_ready, SET * (2 * b + 1) + 2)
                pool.wait_ge(y_lo_ready, KZ * STAGES * b + KZ)
                y_sum(Y11[odd], Y12, Y11[odd])
                pool.wait_ge(w_ready, SET * (2 * b + 2))
                pool.wait_ge(y_summed, 4 * b + 1)
                y_sum(YT, Y22, Y11[odd])
                pool.wait_ge(y_summed, 4 * b + 2)
                y_sum(Y12, Y22, Y12)
                pool.wait_ge(y_lo_ready, KZ * (STAGES * b + z_order(b).index(1) + 1))
                y_sum(YT, Y21[odd], YT)

            y_sums(0, 0)
            pool.wait_ge(consts_ready, 1)
            pool.wait_ge(gn_landed, 32)
            channel_factors(0)
            y_sums(1, 1)
            with pool.Fori(1, NB // 2 - 1) as c:
                channel_factors(2 * c - 1)
                y_sums(2 * c, 0)
                channel_factors(2 * c)
                y_sums(2 * c + 1, 1)
            channel_factors(LAST - 2)
            y_sums(LAST - 1, 0)
            channel_factors(LAST - 1)
            y_sums(LAST, 1)
            pool.wait_ge(y_lo_ready, KZ * (STAGES * LAST + 4))
            for j in range(4, STAGES):
                for k in range(KZ):
                    slot = 2 * ((j + 1) % 2) + k
                    pool.wait_ge(y_hi_ready, KZ * (STAGES * LAST + j) + k + 1)
                    nc.gpsimd.tensor_tensor(y_lo[:, slot, :], (Y11[1], YT, Y22)[j - 4][:, k, :],
                                            y_hi[:, slot, :].bitcast(FP32), ALU.subtract).then_inc(y_lo_ready, 1)
            channel_factors(LAST)


_OUT_SHAPE = (NB, CIN, 32, 32)


def kernel(x, L0_conv_Wt, L0_conv_Wp, L0_conv_Wg, L0_conv_Wz, L0_conv_gn_w, L0_conv_gn_b):
    import numpy as _np
    import concourse.bacc as _bacc
    from concourse import mybir as _mybir
    from concourse.bass_utils import run_bass_kernel_spmd as _run

    nc = _bacc.Bacc("TRN2", target_bir_lowering=False, num_devices=1)
    given = {
        "x": x,
        "wt_t": _np.transpose(L0_conv_Wt),
        "wpg_t": _np.transpose(_np.stack([_np.reshape(w, (2, 2, P, CIN)) for w in (L0_conv_Wp, L0_conv_Wg)], 2),
                               (4, 0, 1, 2, 3)).reshape(CIN, 2, 4 * P),
        "wz": L0_conv_Wz,
        "wz_t": _np.transpose(L0_conv_Wz),
        "gn_w": _np.transpose(_np.reshape(L0_conv_gn_w, (MZ, P))),
        "gn_b": _np.transpose(_np.reshape(L0_conv_gn_b, (MZ, P))),
    }
    arrays = {f"in_{name}_dram": _np.ascontiguousarray(a) for name, a in given.items()}
    args = [nc.dram_tensor(name, a.shape, _mybir.dt.from_np(a.dtype), kind="ExternalInput").ap()
            for name, a in arrays.items()]
    out = nc.dram_tensor("out_0_dram", _OUT_SHAPE, FP32, kind="ExternalOutput").ap()
    rbf_nonlocal_block(nc, *args, out)
    r = _run(nc, [arrays], core_ids=[0])
    return r.results[0]["out_0_dram"]
```
